# Optimizing a Trainium2 kernel written in Bass

```python
import numpy as np
import jax
import jax.numpy as jnp

def _softmax(x, axis=-1):
    return jax.nn.softmax(x, axis=axis)

def _gelu(x):
    return jax.nn.gelu(x, approximate=True)

def _silu(x):
    return jax.nn.silu(x)

def _sigmoid(x):
    return jax.nn.sigmoid(x)

def _layernorm(x, axis=-1, eps=1e-05):
    m = jnp.mean(x, axis=axis, keepdims=True)
    v = jnp.var(x, axis=axis, keepdims=True)
    return (x - m) / jnp.sqrt(v + eps)

def _scatter_add(tgt, idx, src, axis=0):
    return tgt.at[idx].add(src)

def _segment_sum(src, seg, n):
    return jax.ops.segment_sum(src, seg, n)
kernel_name = 'mk_conv_seq_d2_conv_nchw96_r4_8a7427'

def setup_inputs(seed: int=0):
    np.random.seed(seed)
    _w = jnp.asarray

    def _rec_inputs():
        import jax
        import jax.numpy as jnp
        _gk = jax.random.key(seed)
        x = 7.572e-06 + 1 * jax.random.normal(jax.random.fold_in(_gk, 1), (32, 24, 56, 56), jnp.float32)
        return x
    x = _rec_inputs()

    def _L0_conv_setup():
        import jax, jax.numpy as jnp
        import numpy as np
        LN_EPS = 1e-05
        key = jax.random.key(seed)
        ks = jax.random.split(key, 8)
        dim, B, H, W = (24, 32, 56, 56)
        return {'x': jax.random.normal(ks[0], (B, dim, H, W), jnp.float32), 'conv_w': jax.random.normal(ks[1], (dim, 1, 7, 7), jnp.float32) * 0.05, 'conv_b': jax.random.normal(ks[2], (dim,), jnp.float32) * 0.05, 'ln_g': jnp.ones((dim,), jnp.float32), 'ln_b': jnp.zeros((dim,), jnp.float32), 'w1': jax.random.normal(ks[3], (dim, 4 * dim), jnp.float32) * 0.05, 'b1': jax.random.normal(ks[4], (4 * dim,), jnp.float32) * 0.05, 'w2': jax.random.normal(ks[5], (4 * dim, dim), jnp.float32) * 0.05, 'b2': jax.random.normal(ks[6], (dim,), jnp.float32) * 0.05, 'layer_scale': jnp.ones((dim, 1, 1), jnp.float32)}
    _L0_conv_all = _L0_conv_setup()
    _L0_conv_in = {k: v for k, v in _L0_conv_all.items() if k in ('conv_w', 'conv_b', 'ln_g', 'ln_b', 'w1', 'b1', 'w2', 'b2', 'layer_scale')}
    del _L0_conv_all

    def _L1_conv_setup():
        import jax, jax.numpy as jnp
        import numpy as np
        WS = 8
        K = 9
        BN_EPS = 1e-05

        def conv1x1(x, w, b):
            return jnp.einsum('bchw,oc->bohw', x, w) + b[None, :, None, None]

        def affine(x, s, t):
            return x * s[None, :, None, None] + t[None, :, None, None]

        def window_partition(x, ws):
            B, C, H, W = x.shape
            x = x.reshape(B, C, H // ws, ws, W // ws, ws)
            x = x.transpose(0, 2, 4, 1, 3, 5)
            return x.reshape(-1, C, ws, ws)

        def window_reverse(win, ws, B, H, W):
            C = win.shape[1]
            x = win.reshape(B, H // ws, W // ws, C, ws, ws)
            x = x.transpose(0, 3, 1, 4, 2, 5)
            return x.reshape(B, C, H, W)

        def knn_idx(nodes, k):
            nrm = jnp.maximum(jnp.linalg.norm(nodes, axis=-1, keepdims=True), 1e-12)
            xn = nodes / nrm
            sq = jnp.sum(xn * xn, axis=-1, keepdims=True)
            dist = sq - 2.0 * jnp.einsum('bnc,bmc->bnm', xn, xn) + sq.transpose(0, 2, 1)
            _, idx = jax.lax.top_k(-dist, k)
            return idx
        key = jax.random.key(seed)
        ks = jax.random.split(key, 16)
        B, C, H, W = (16, 24, 16, 16)
        O = 2 * C

        def bn(k1, k2, n):
            g = 1.0 + 0.1 * jax.random.normal(k1, (n,), jnp.float32)
            b = 0.1 * jax.random.normal(k2, (n,), jnp.float32)
            return (g, b)
        x = jax.random.normal(ks[0], (B, C, H, W), jnp.float32)
        fc1_w = 0.05 * jax.random.normal(ks[1], (C, C), jnp.float32)
        fc1_b = 0.02 * jax.random.normal(ks[2], (C,), jnp.float32)
        fc1_s, fc1_t = bn(ks[3], ks[4], C)
        ew = 0.05 * jax.random.normal(ks[5], (O, 2 * C), jnp.float32)
        eb = 0.02 * jax.random.normal(ks[6], (O,), jnp.float32)
        es, et = bn(ks[7], ks[8], O)
        fc2_w = 0.05 * jax.random.normal(ks[9], (C, O), jnp.float32)
        fc2_b = 0.02 * jax.random.normal(ks[10], (C,), jnp.float32)
        fc2_s, fc2_t = bn(ks[11], ks[12], C)
        return {'x': x, 'fc1_w': fc1_w, 'fc1_b': fc1_b, 'fc1_s': fc1_s, 'fc1_t': fc1_t, 'ew': ew, 'eb': eb, 'es': es, 'et': et, 'fc2_w': fc2_w, 'fc2_b': fc2_b, 'fc2_s': fc2_s, 'fc2_t': fc2_t}
    _L1_conv_all = _L1_conv_setup()
    _L1_conv_in = {k: v for k, v in _L1_conv_all.items() if k in ('fc1_w', 'fc1_b', 'fc1_s', 'fc1_t', 'ew', 'eb', 'es', 'et', 'fc2_w', 'fc2_b', 'fc2_s', 'fc2_t')}
    del _L1_conv_all
    return {'x': x, 'L0_conv_conv_w': _L0_conv_in['conv_w'], 'L0_conv_conv_b': _L0_conv_in['conv_b'], 'L0_conv_ln_g': _L0_conv_in['ln_g'], 'L0_conv_ln_b': _L0_conv_in['ln_b'], 'L0_conv_w1': _L0_conv_in['w1'], 'L0_conv_b1': _L0_conv_in['b1'], 'L0_conv_w2': _L0_conv_in['w2'], 'L0_conv_b2': _L0_conv_in['b2'], 'L0_conv_layer_scale': _L0_conv_in['layer_scale'], 'L1_conv_fc1_w': _L1_conv_in['fc1_w'], 'L1_conv_fc1_b': _L1_conv_in['fc1_b'], 'L1_conv_fc1_s': _L1_conv_in['fc1_s'], 'L1_conv_fc1_t': _L1_conv_in['fc1_t'], 'L1_conv_ew': _L1_conv_in['ew'], 'L1_conv_eb': _L1_conv_in['eb'], 'L1_conv_es': _L1_conv_in['es'], 'L1_conv_et': _L1_conv_in['et'], 'L1_conv_fc2_w': _L1_conv_in['fc2_w'], 'L1_conv_fc2_b': _L1_conv_in['fc2_b'], 'L1_conv_fc2_s': _L1_conv_in['fc2_s'], 'L1_conv_fc2_t': _L1_conv_in['fc2_t']}

def reference(x, L0_conv_conv_w, L0_conv_conv_b, L0_conv_ln_g, L0_conv_ln_b, L0_conv_w1, L0_conv_b1, L0_conv_w2, L0_conv_b2, L0_conv_layer_scale, L1_conv_fc1_w, L1_conv_fc1_b, L1_conv_fc1_s, L1_conv_fc1_t, L1_conv_ew, L1_conv_eb, L1_conv_es, L1_conv_et, L1_conv_fc2_w, L1_conv_fc2_b, L1_conv_fc2_s, L1_conv_fc2_t):
    import jax
    import jax.numpy as jnp

    def _L0_conv_ref(x, conv_w, conv_b, ln_g, ln_b, w1, b1, w2, b2, layer_scale):
        import jax, jax.numpy as jnp
        import numpy as np
        LN_EPS = 1e-05
        dim = x.shape[1]
        h = jax.lax.conv_general_dilated(x, conv_w, window_strides=(1, 1), padding=((3, 3), (3, 3)), dimension_numbers=('NCHW', 'OIHW', 'NCHW'), feature_group_count=dim)
        h = h + conv_b[None, :, None, None]
        h = jnp.transpose(h, (0, 2, 3, 1))
        mu = jnp.mean(h, axis=-1, keepdims=True)
        var = jnp.var(h, axis=-1, keepdims=True)
        h = (h - mu) * jax.lax.rsqrt(var + LN_EPS) * ln_g + ln_b
        h = jax.nn.gelu(jnp.einsum('bhwc,cf->bhwf', h, w1) + b1, approximate=False)
        h = jnp.einsum('bhwf,fc->bhwc', h, w2) + b2
        h = jnp.transpose(h, (0, 3, 1, 2)) * layer_scale[None]
        return h + x

    def _L1_conv_ref(x, fc1_w, fc1_b, fc1_s, fc1_t, ew, eb, es, et, fc2_w, fc2_b, fc2_s, fc2_t):
        import jax, jax.numpy as jnp
        import numpy as np
        WS = 8
        K = 9
        BN_EPS = 1e-05

        def conv1x1(x, w, b):
            return jnp.einsum('bchw,oc->bohw', x, w) + b[None, :, None, None]

        def affine(x, s, t):
            return x * s[None, :, None, None] + t[None, :, None, None]

        def window_partition(x, ws):
            B, C, H, W = x.shape
            x = x.reshape(B, C, H // ws, ws, W // ws, ws)
            x = x.transpose(0, 2, 4, 1, 3, 5)
            return x.reshape(-1, C, ws, ws)

        def window_reverse(win, ws, B, H, W):
            C = win.shape[1]
            x = win.reshape(B, H // ws, W // ws, C, ws, ws)
            x = x.transpose(0, 3, 1, 4, 2, 5)
            return x.reshape(B, C, H, W)

        def knn_idx(nodes, k):
            nrm = jnp.maximum(jnp.linalg.norm(nodes, axis=-1, keepdims=True), 1e-12)
            xn = nodes / nrm
            sq = jnp.sum(xn * xn, axis=-1, keepdims=True)
            dist = sq - 2.0 * jnp.einsum('bnc,bmc->bnm', xn, xn) + sq.transpose(0, 2, 1)
            _, idx = jax.lax.top_k(-dist, k)
            return idx
        B, C, H, W = x.shape
        tmp = x
        y = affine(conv1x1(x, fc1_w, fc1_b), fc1_s, fc1_t)
        win = window_partition(y, WS)
        Bw = win.shape[0]
        nodes = win.reshape(Bw, C, WS * WS).transpose(0, 2, 1)
        idx = jax.lax.stop_gradient(knn_idx(nodes, K))
        x_j = jax.vmap(lambda n, i: n[i])(nodes, idx)
        x_i = nodes[:, :, None, :]
        feat = jnp.concatenate([jnp.broadcast_to(x_i, x_j.shape), x_j - x_i], axis=-1)
        h = jnp.einsum('bnkc,oc->bnko', feat, ew) + eb
        h = h * es + et
        h = jax.nn.gelu(h, approximate=False)
        h = jnp.max(h, axis=2)
        O = h.shape[-1]
        win_out = h.transpose(0, 2, 1).reshape(Bw, O, WS, WS)
        y = window_reverse(win_out, WS, B, H, W)
        y = affine(conv1x1(y, fc2_w, fc2_b), fc2_s, fc2_t)
        return y + tmp

    def _gn(v, G=32, eps=1e-05):
        B_, C_, H_, W_ = v.shape
        g = v.reshape(B_, G, C_ // G, H_, W_)
        m = jnp.mean(g, axis=(2, 3, 4), keepdims=True)
        s = jnp.var(g, axis=(2, 3, 4), keepdims=True)
        return ((g - m) / jnp.sqrt(s + eps)).reshape(v.shape)

    def _ln_c(v, eps=1e-06):
        m = jnp.mean(v, axis=1, keepdims=True)
        s = jnp.var(v, axis=1, keepdims=True)
        return (v - m) / jnp.sqrt(s + eps)

    def _ln_t(v, eps=1e-05):
        m = jnp.mean(v, axis=-1, keepdims=True)
        s = jnp.var(v, axis=-1, keepdims=True)
        return (v - m) / jnp.sqrt(s + eps)

    def _to_tokens(v):
        B_, C_, H_, W_ = v.shape
        return v.reshape(B_, C_, H_ * W_).transpose(0, 2, 1)

    def _from_tokens(t, like):
        B_, C_, H_, W_ = like.shape
        return t.transpose(0, 2, 1).reshape(B_, C_, H_, W_)
    x = _L0_conv_ref(x, L0_conv_conv_w, L0_conv_conv_b, L0_conv_ln_g, L0_conv_ln_b, L0_conv_w1, L0_conv_b1, L0_conv_w2, L0_conv_b2, L0_conv_layer_scale)
    x = _L1_conv_ref(x, L1_conv_fc1_w, L1_conv_fc1_b, L1_conv_fc1_s, L1_conv_fc1_t, L1_conv_ew, L1_conv_eb, L1_conv_es, L1_conv_et, L1_conv_fc2_w, L1_conv_fc2_b, L1_conv_fc2_s, L1_conv_fc2_t)
    return x

_drawn_inputs = setup_inputs


def setup_inputs(seed=0):
    import zlib

    import numpy as np

    out = dict(_drawn_inputs(seed))
    spreads = {'L0_conv_ln_g': (1.0, 0.6), 'L0_conv_ln_b': (0.0, 0.8), 'L0_conv_layer_scale': (1.0, 0.6)}
    factors = {'L0_conv_conv_b': 6.103,
     'L0_conv_b1': 4.429,
     'L1_conv_fc1_w': 3.466,
     'L1_conv_fc1_b': 8.0,
     'L1_conv_fc1_s': 8.0,
     'L1_conv_fc1_t': 8.0,
     'L1_conv_ew': 3.184,
     'L1_conv_eb': 27.186,
     'L1_conv_es': 8.0,
     'L1_conv_et': 28.544,
     'L1_conv_fc2_s': 8.0,
     'L1_conv_fc2_b': 63.76,
     'L1_conv_fc2_t': 64.0}
    for name, (base, spread) in spreads.items():
        noise = np.random.default_rng([zlib.crc32(name.encode()), seed]).standard_normal(out[name].shape)
        drawn = base * np.exp(spread * noise) if base else spread * noise
        out[name] = jnp.asarray(drawn.astype(out[name].dtype))
    for name, factor in factors.items():
        out[name] = (out[name] * factor).astype(out[name].dtype)
    return out
```

```python
import concourse.bass as bass
import concourse.mybir as mybir
from contextlib import ExitStack

B, C, HW = 32, 24, 56
F = 4 * C
O = 2 * C
KS = 7
PAD = KS // 2
WS = 8
NN = WS * WS
NB = 8
IMG = HW * HW
CHAN = C * IMG

G = 4
Q = B // (2 * G)
SR = WS
L = SR * HW
NS = HW // SR
NI = Q * NS
NSTEP = 2 * NI
WX = HW // WS
NU = NI * WX
CP = C // 2
ZL = 2 * HW - 1
NEG = -1.0e30
TAKEN = 1.0e30

COLS = {}
_at = 0
for _name, _n in (("center", 128), ("mean", 128), ("norm", 128), ("halfsq", 128), ("ident", 128), ("prefix", 128),
                  ("negi", NN), ("i2", NN), ("maskc", 1),
                  ("w1", G * F), ("w2", 3 * 128), ("ls_row", 128), ("ln_g", 1), ("ln_b", 1), ("b1", 3), ("b2", 1), ("ls", 1),
                  ("conv_b", CP),
                  ("fc1", 128), ("s1", 1), ("b1f", 1), ("t1", 1),
                  ("wb", G * O), ("es_row", O), ("wa_q", G * 4 * O), ("wb_q", G * 4 * O),
                  ("eb", 1), ("es", 1), ("et", 1), ("fc2", 64), ("s2_row", 64), ("s2", 1), ("b2f", 1), ("t2", 1)):
    COLS[_name] = (_at, _n)
    _at += _n
NCOL = _at


def build(nc, x, zfilt, params, out):
    F32, BF = mybir.dt.float32, mybir.dt.bfloat16
    ALU, ACT = mybir.AluOpType, mybir.ActivationFunctionType
    ctx = ExitStack()
    with ctx:
        def sb(name, shape, dt=F32):
            return ctx.enter_context(nc.sbuf_tensor(name, shape, dt))

        def sem(name):
            return ctx.enter_context(nc.semaphore(name))

        def at_least(eng, s, count):
            if isinstance(count, int) and count <= 0:
                return
            eng.wait_ge(s, count)

        conv_d = nc.dram_tensor("conv_d", (C, HW, B, HW), F32, kind="Internal").ap()
        x1_d = nc.dram_tensor("x1_d", (NI, G, 2 * C, L), F32, kind="Internal").ap()

        par = sb("par", [128, NCOL])

        def P(name):
            a, n = COLS[name]
            return par[:, a:a + n]

        KC = 2 * HW
        toep = [sb(f"toep{i}", [KC, KS, KC]) for i in range(2)]
        xrow = [sb(f"xrow{i}", [KC, B, HW + 2 * PAD]) for i in range(2)]
        cvo = [sb(f"cvo{i}", [KC, B * HW]) for i in range(2)]
        NBUF = 4
        ht = sb("ht", [128, NBUF, L])
        xt = sb("xt", [128, NBUF, L])
        x1o = sb("x1o", [128, NBUF, L])
        sq = sb("sq", [128, L])
        ve = sb("ve", [128, L])
        rs = sb("rs", [128, L])
        hn = sb("hn", [128, 2, L])
        gl = sb("gl", [128, 3, L])
        w1g = sb("w1g", [128, 3, 128])
        w2s = sb("w2s", [128, 3, 128])
        b1s = sb("b1s", [128, 3])
        b2s = sb("b2s", [128, 1])
        mhalf = sb("mhalf", [128, 2 * L])
        c1 = sb("c1", [128, 1])
        wp = sb("wp", [128, G * O])
        wq = sb("wq", [128, G, 2, 2 * O])
        gb = sb("gb", [128, 1])
        f2 = sb("f2", [128, 64])
        c2 = sb("c2", [128, 1])
        identb = sb("identb", [128, 128], BF)
        nidentb = sb("nidentb", [128, 128], BF)
        prefb = sb("prefb", [128, 128], BF)
        negb = sb("negb", [128, G, NN], BF)
        i2b = sb("i2b", [128, NN], BF)
        x1t = ht[:, :, :].rearrange("p (b u) l -> p b u l", b=2)
        x1r = xt[:, :, :].rearrange("p (b u) l -> p b u l", b=2)
        outs = x1o[:, :, :].rearrange("p (b u) l -> p b u l", b=2)
        yb = sb("yb", [128, 2, WX, 2, NN])
        xa = sb("xa", [128, 2, 2, L])
        xb = sb("xb", [128, 2, L])
        xbm = sb("xbm", [128, 2, 2, WX, G, NN])
        sq2 = sb("sq2", [128, 2, L])
        nv = sb("nv", [128, 2, L])
        rn = sb("rn", [128, 2, L])
        t8 = sb("t8", [128, 2 * G, NB])
        wsel = sb("wsel", [128, G, NN], BF)
        msk = sb("msk", [128, 2, G, NN], BF)
        mts = sb("mts", [128, G * NN], BF)
        slot = sb("slot", [128, 2, G, NN], BF)
        onehot = sb("onehot", [128, 2, G, NB, NN], BF)
        pb = sb("pb", [128, 2, 3, G, 2 * O], BF)
        red = sb("red", [2 * O, 2, 2, G, NN])
        red9 = sb("red9", [2 * O, 2, G, NN])
        qs = sb("qs", [2 * O, 2, G, NN])
        hq = sb("hq", [2 * O, 2, G, NN])
        gg = sb("gg", [2 * O, 2, G, NN])
        og = sb("og", [2 * O, 2, G, SR, WX, WS])

        bank = ctx.enter_context(nc.psum_tensor("bank", [128, 8, 512], F32))

        par_in, zeroed, mhalf_set, ready, lnb_dot = sem("par_in"), sem("zeroed"), sem("mhalf_set"), sem("ready"), sem("lnb_dot")
        conv_in = [sem(f"conv_in{i}") for i in range(2)]
        conv_mm = sem("conv_mm")
        conv_evac_a, conv_evac_v = sem("conv_evac_a"), sem("conv_evac_v")
        conv_out = [sem(f"conv_out{i}") for i in range(2)]
        h_in = [sem(f"h_in{i}") for i in range(NBUF)]
        x_in = [sem(f"x_in{i}") for i in range(NBUF)]
        x1_out = [sem(f"x1_out{i}") for i in range(NBUF)]
        ctr_d, var_d, mm1_d, mm2_d = sem("ctr_d"), sem("var_d"), sem("mm1_d"), sem("mm2_d")
        sq_d, gelu_d, ve_d, pow_d, hn_d, x1_dn = (sem("sq_d"), sem("gelu_d"), sem("ve_d"), sem("pow_d"), sem("hn_d"),
                                                  sem("x1_dn"))
        s = {}
        for name in ("fc1_mm", "y_done", "ysq_done", "norm_mm", "nv_done", "rn_done", "xa_done", "xasq_done", "half_mm",
                     "xb_done", "xbm_done", "dist_mm", "p_mm", "hi_done", "res1_mm", "mid_done", "res2_mm", "lo_done", "t8_done",
                     "rep_done", "mask_done", "mt_mm", "mts_done", "slot_mm", "slot_done", "onehot_done", "gat_mm",
                     "red_done", "self_mm", "node_done", "q_done", "addq_done",
                     "geg_done", "og_done", "fc2_mm", "fin_done"):
            s[name] = sem("g_" + name)
        x1t_in = [sem(f"x1t_in{i}") for i in range(2)]
        x1r_in = [sem(f"x1r_in{i}") for i in range(2)]
        final_out = [sem(f"final_out{i}") for i in range(2)]

        CH = 4
        CL = B // CH * HW
        block = ctx.enter_context(nc.Block())

        @block.sync
        def _(sp):
            sp.dma_start(par[:, :], params).then_inc(par_in, 16)
            sp.wait_ge(zeroed, 1)

            def load_pair(cp, b):
                for k in range(2):
                    sp.dma_start(xrow[b][k * HW:(k + 1) * HW, :, PAD:PAD + HW],
                                 x[:, 2 * cp + k, :, :].rearrange("b h w -> h b w")).then_inc(conv_in[b], 16)
                    src = zfilt[2 * cp + k, :, 0:HW]
                    band = bass.AP(tensor=src.tensor, offset=src.offset, ap=[[1, HW], [ZL, KS], [1, HW]])
                    sp.dma_start(toep[b][k * HW:(k + 1) * HW, :, k * HW:(k + 1) * HW], band
                                 ).then_inc(conv_in[b], 16)

            def store_pair(cp, b, n):
                sp.wait_ge(conv_evac_a, 2 * (n + 1))
                sp.wait_ge(conv_evac_v, 2 * (n + 1))
                sp.dma_start(conv_d[bass.ds(2 * cp, 2), :, :, :].rearrange("c h b w -> (c h) (b w)"), cvo[b][:, :]
                             ).then_inc(conv_out[b], 16)

            load_pair(0, 0)
            load_pair(1, 1)
            with sp.Fori(0, CP // 2 - 1) as j:
                for b in range(2):
                    sp.wait_ge(conv_mm, 2 * j + b + 1)
                    load_pair(2 * j + b + 2, b)
                    store_pair(2 * j + b, b, 2 * j + b)
            for b in range(2):
                store_pair(CP - 2 + b, b, CP - 2 + b)
            for b in range(2):
                sp.wait_ge(conv_out[b], 16 * (CP // 2))

            sp.wait_ge(zeroed, 2)

            def load_step(m, r):
                i, u = m // 2, r % 2
                q, st = i // NS, i % NS
                at_least(sp, ctr_d, m - NBUF + 1)
                for g in range(G):
                    sp.dma_start(ht[32 * g:32 * g + C, r, :].rearrange("p (h w) -> p h w", w=HW),
                                 conv_d[:, bass.ds((NS - 1) * SR - SR * st, SR), 8 * q + 2 * g + u, :]).then_inc(h_in[r], 16)
                at_least(sp, x1_dn, m - NBUF + 1)
                for g in range(G):
                    sp.dma_start(xt[32 * g:32 * g + C, r, :],
                                 x[8 * q + 2 * g + u, :, bass.ts(st, SR), :].rearrange("c h w -> c (h w)")
                                 ).then_inc(x_in[r], 16)

            def store_step(m, r):
                i, u = m // 2, r % 2
                sp.wait_ge(x1_dn, m + 1)
                for g in range(G):
                    sp.dma_start(x1_d[i, g, u * C:(u + 1) * C, :], x1o[32 * g:32 * g + C, r, :]).then_inc(x1_out[r], 16)

            for r in range(NBUF):
                load_step(r, r)
            with sp.Fori(0, NSTEP // NBUF - 1) as j:
                for r in range(NBUF):
                    store_step(NBUF * j + r, r)
                    load_step_m = NBUF * j + (NBUF + r)
                    load_step(load_step_m, r)
            for r in range(NBUF):
                store_step(NSTEP - NBUF + r, r)
            for r in range(NBUF):
                sp.wait_ge(x1_out[r], 16 * G * (NSTEP // NBUF))

            def load_iter(i, b):
                at_least(sp, s["fc1_mm"], 2 * (i - 1))
                for g in range(G):
                    sp.dma_start(x1t[32 * g:32 * g + C, b, :, :],
                                 x1_d[i, g, :, :].rearrange("(u c) l -> c u l", u=2)).then_inc(x1t_in[b], 16)

            def load_res(i, b):
                at_least(sp, s["fin_done"], 2 * (i - 1))
                for h in range(2):
                    sp.dma_start(x1r[64 * h:64 * h + 2 * C, b, :, :],
                                 x1_d[i, h:G:2, :, :].rearrange("g p l -> p g l")).then_inc(x1r_in[b], 16)

            def store_iter(i, b):
                q, st = i // NS, i % NS
                sp.wait_ge(s["fin_done"], 2 * (i + 1))
                for h in range(2):
                    for gp in range(2):
                        dst = out[bass.ds(8 * q + 4 * gp + 2 * h, 2), :, bass.ts(st, SR), :]
                        sp.dma_start(dst.rearrange("b c h w -> (b c) (h w)"), outs[64 * h:64 * h + 2 * C, b, gp, :]
                                     ).then_inc(final_out[b], 16)

            for b in range(2):
                load_iter(b, b)
                load_res(b, b)
            with sp.Fori(0, NI // 2 - 1) as j:
                for b in range(2):
                    load_iter(2 * j + (b + 2), b)
                    store_iter(2 * j + b, b)
                    load_res(2 * j + (b + 2), b)
            for b in range(2):
                store_iter(NI - 2 + b, b)
            for b in range(2):
                sp.wait_ge(final_out[b], 64 * (NI // 2))

        @block.gpsimd
        def _(pool):
            for b in range(2):
                nc.gpsimd.memset(toep[b][:, :, :], 0.0)
                last = nc.gpsimd.memset(xrow[b][:, :, :], 0.0)
            last.then_inc(zeroed, 1)
            nc.gpsimd.memset(mhalf[:, :], -0.5).then_inc(mhalf_set, 1)
            for t in (ht, xt):
                last = nc.gpsimd.memset(t[:, :, :], 0.0)
            last.then_inc(zeroed, 1)
            nc.gpsimd.memset(xbm[:, :, :, :, :, :], 0.0)
            nc.gpsimd.memset(pb[:, :, :, :, :], 0.0).then_inc(zeroed, 1)
            pool.wait_ge(mhalf_set, 1)

            with pool.Fori(0, NSTEP) as m:
                pool.wait_ge(ve_d, m + 1)
                pool.wait_ge(hn_d, m)
                nc.gpsimd.tensor_tensor(rs[:, :], ve[:, :], mhalf[:, 0:L], ALU.pow).then_inc(pow_d, 1)

            def inv_norm(i):
                pool.wait_ge(s["nv_done"], 2 * (i + 1))
                at_least(pool, s["xa_done"], i)
                nc.gpsimd.tensor_tensor(rn[:, :, :], nv[:, :, :], mhalf[:, :].rearrange("p (u l) -> p u l", u=2),
                                        ALU.pow).then_inc(s["rn_done"], 1)

            def add_q(n, k):
                pool.wait_ge(s["q_done"], n + 1)
                pool.wait_ge(s["node_done"], n + 1)
                at_least(pool, s["geg_done"], n)
                nc.gpsimd.tensor_tensor(hq[:, :, :, :].rearrange("p h g i -> p h (g i)"),
                                        red9[:, :, :, :].rearrange("p h g i -> p h (g i)"),
                                        qs[:, k, :, :].rearrange("p g i -> p (g i)").unsqueeze(1).broadcast_to(
                                            [2 * O, 2, G * NN]), ALU.add).then_inc(s["addq_done"], 1)

            def pool_slot(n, i, r, add=True, pre=True):
                if add:
                    add_q(n - 1, (r + 1) % 2)
                if pre and r % WX == 1:
                    inv_norm(i + 1)

            inv_norm(0)
            for r in range(2 * WX):
                pool_slot(r, r // WX, r, add=r > 0)
            with pool.Fori(1, NI // 2 - 1) as j:
                for r in range(2 * WX):
                    pool_slot(2 * WX * j + r, 2 * j + r // WX, r)
            for r in range(2 * WX):
                pool_slot(NU - 2 * WX + r, NI - 2 + r // WX, r, pre=r < WX)
            add_q(NU - 1, 1)

        @block.scalar
        def _(act):
            act.wait_ge(par_in, 16)
            with act.Fori(0, CP // 2) as j:
                for b in range(2):
                    act.wait_ge(conv_mm, 2 * j + b + 1)
                    act.wait_ge(conv_out[b], 16 * j)
                    for ch in range(2):
                        nc.scalar.activation(cvo[b][:, ch * CL:(ch + 1) * CL], bank[0:KC, 4 * b + ch, 0:CL], ACT.Identity,
                                             bias=P("conv_b")[0:KC, bass.ds(2 * j + b, 1)], scale=1.0
                                             ).then_inc(conv_evac_a, 1)

            def square(m, r):
                act.wait_ge(ctr_d, m + 1)
                nc.scalar.activation(sq[:, :], bank[:, r % 2, 0:L], ACT.Square).then_inc(sq_d, 1)

            def gelu(m, r):
                for t in range(3):
                    act.wait_ge(mm1_d, 3 * m + (t + 1))
                    nc.scalar.activation(gl[:, t, :], bank[:, 3 + t, 0:L], ACT.Gelu, bias=b1s[:, t:t + 1], scale=1.0
                                         ).then_inc(gelu_d, 1)

            act.wait_ge(ready, 1)
            act.wait_ge(zeroed, 3)
            square(0, 0)
            with act.Fori(0, NSTEP // 2 - 1) as j:
                for r in range(2):
                    square(2 * j + (r + 1), r + 1)
                    gelu(2 * j + r, r)
            square(NSTEP - 1, 1)
            gelu(NSTEP - 2, 0)
            gelu(NSTEP - 1, 1)

            def make_y(i, b):
                for u in range(2):
                    act.wait_ge(s["fc1_mm"], 2 * i + (u + 1))
                    nc.scalar.activation(yb[:, b, :, u, :], bank[:, 6 + u, 0:L].rearrange("p (w i) -> p w i", w=WX), ACT.Identity, bias=c1[:, 0:1],
                                         scale=P("s1")).then_inc(s["y_done"], 1)
                act.wait_ge(s["y_done"], 2 * (i + 1))
                nc.scalar.activation(sq2[:, :, :].rearrange("p u (w i) -> p u w i", w=WX),
                                     yb[:, b, :, :, :].rearrange("p w u i -> p u w i"), ACT.Square).then_inc(s["ysq_done"], 1)

            def square_xa(i, b):
                act.wait_ge(s["xa_done"], i + 1)
                act.wait_ge(s["norm_mm"], 2 * (i + 1))
                nc.scalar.activation(sq2[:, :, :], xa[:, b, :, :], ACT.Square).then_inc(s["xasq_done"], 1)

            def spread_xb(i, b):
                act.wait_ge(s["xb_done"], 2 * (i + 1))
                at_least(act, s["dist_mm"], WX * (i - 1))
                for g in range(G):
                    last = nc.scalar.copy(xbm[32 * g:32 * g + 32, b, :, :, g, :],
                                          xb[32 * g:32 * g + 32, :, :].rearrange("p u (w i) -> p u w i", w=WX))
                last.then_inc(s["xbm_done"], 1)

            def split(n, k, part, waits, done):
                act.wait_ge(waits, n + 1)
                src = bank[:, 3, 0:G * O].rearrange("p (g o) -> p g o", g=G)
                for u in range(2):
                    last = nc.scalar.copy(pb[64 * u:64 * u + 64, k, part, :, u * O:(u + 1) * O],
                                          src[64 * u:64 * u + 64, :, :])
                last.then_inc(done, 1)

            def act_slot(n, i, r, gather=True, add=True, ahead1=True, pre=True):
                wx, b = r % WX, r // WX
                if ahead1:
                    split(n + 1, (r + 1) % 2, 0, s["p_mm"], s["hi_done"])
                if ahead1:
                    split(n + 1, (r + 1) % 2, 1, s["res1_mm"], s["mid_done"])
                if ahead1:
                    act.wait_ge(s["mt_mm"], n + 2)
                    nc.scalar.copy(mts[:, :], bank[:, 4, 0:G * NN]).then_inc(s["mts_done"], 1)
                    split(n + 1, (r + 1) % 2, 2, s["res2_mm"], s["lo_done"])
                if ahead1:
                    act.wait_ge(s["slot_mm"], n + 2)
                    nc.scalar.copy(slot[:, (r + 1) % 2, :, :].rearrange("p g i -> p (g i)"),
                                   bank[:, 4, G * NN:2 * G * NN]).then_inc(s["slot_done"], 1)
                if gather:
                    act.wait_ge(s["self_mm"], n + 1)
                    at_least(act, s["addq_done"], n - 1)
                    nc.scalar.copy(qs[:, r % 2, :, :].rearrange("p g i -> p (g i)"), bank[0:2 * O, 5, G * NN:2 * G * NN]
                                   ).then_inc(s["q_done"], 1)
                if add:
                    act.wait_ge(s["addq_done"], n)
                    at_least(act, s["og_done"], n - 1)
                    nc.scalar.activation(gg[:, :, :, :], hq[:, :, :, :], ACT.Gelu, bias=gb[0:2 * O, 0:1], scale=1.0
                                         ).then_inc(s["geg_done"], 1)
                if pre and wx == 0:
                    make_y(i + 1, (b + 1) % 2)
                if pre and wx == 2:
                    square_xa(i + 1, (b + 1) % 2)
                if pre and wx == 4:
                    spread_xb(i + 1, (b + 1) % 2)

            make_y(0, 0)
            square_xa(0, 0)
            spread_xb(0, 0)
            act_slot(-1, -1, 13, gather=False, add=False, pre=False)
            for r in range(2 * WX):
                act_slot(r, r // WX, r, add=r > 0)
            with act.Fori(1, NI // 2 - 1) as j:
                for r in range(2 * WX):
                    act_slot(2 * WX * j + r, 2 * j + r // WX, r)
            for r in range(2 * WX):
                n = NU - 2 * WX + r
                act_slot(n, NI - 2 + r // WX, r, ahead1=n + 1 < NU, pre=r < WX)
            act_slot(NU, NI, 0, gather=False, ahead1=False, pre=False)

        @block.vector
        def _(dve):
            dve.wait_ge(par_in, 16)

            with dve.Fori(0, CP // 2) as j:
                for b in range(2):
                    dve.wait_ge(conv_mm, 2 * j + b + 1)
                    dve.wait_ge(conv_out[b], 16 * j)
                    for ch in range(2, 4):
                        nc.vector.tensor_scalar(cvo[b][:, ch * CL:(ch + 1) * CL], bank[0:KC, 4 * b + ch, 0:CL],
                                                P("conv_b")[0:KC, bass.ds(2 * j + b, 1)], None, ALU.add
                                                ).then_inc(conv_evac_v, 1)

            dve.wait_ge(lnb_dot, 1)
            nc.vector.tensor_tensor(b1s[:, :], bank[:, 6, 0:3], P("b1"), ALU.add)
            nc.vector.tensor_scalar(w1g[:, :, :].rearrange("p t m -> p (t m)"), P("w1"), P("ln_g"), None, ALU.mult)
            for t in range(3):
                nc.vector.tensor_tensor(w2s[:, t, :], P("w2")[:, 128 * t:128 * t + 128], P("ls_row"), ALU.mult)
            nc.vector.tensor_tensor(b2s[:, :], P("b2"), P("ls"), ALU.mult)
            nc.vector.scalar_tensor_tensor(c1[:, :], P("b1f"), P("s1"), P("t1"), ALU.mult, ALU.add)
            nc.vector.tensor_tensor(wp[:, :].rearrange("p (g o) -> p g o", g=G), P("wb").rearrange("p (g o) -> p g o", g=G),
                                    P("es_row").unsqueeze(1).broadcast_to([128, G, O]), ALU.mult)
            wqf = wq[:, :, :, :].rearrange("p g u m -> p (g u m)")
            nc.vector.tensor_tensor(wqf, P("wa_q"), P("wb_q"), ALU.subtract).then_inc(s["rep_done"], 1)
            dve.wait_ge(s["rep_done"], 1)
            wqv = wq[:, :, :, :].rearrange("p g u (v o) -> p (g u v) o", v=2)
            nc.vector.tensor_tensor(wqv, wqv, P("es_row").unsqueeze(1).broadcast_to([128, 4 * G, O]), ALU.mult)
            nc.vector.scalar_tensor_tensor(gb[:, :], P("eb"), P("es"), P("et"), ALU.mult, ALU.add)
            nc.vector.tensor_tensor(f2[:, :], P("fc2"), P("s2_row"), ALU.mult)
            nc.vector.scalar_tensor_tensor(c2[:, :], P("b2f"), P("s2"), P("t2"), ALU.mult, ALU.add)
            nc.vector.tensor_copy(identb[:, :], P("ident"))
            nc.vector.tensor_scalar(nidentb[:, :], P("ident"), -1.0, None, ALU.mult)
            nc.vector.tensor_copy(prefb[:, :], P("prefix"))
            nc.vector.tensor_copy(negb[:, :, :], P("negi").unsqueeze(1).broadcast_to([128, G, NN]))
            nc.vector.tensor_copy(i2b[:, :], P("i2")).then_inc(ready, 1)

            dve.wait_ge(ready, 1)
            dve.wait_ge(zeroed, 2)

            def add_eps(m):
                dve.wait_ge(var_d, m + 1)
                at_least(dve, pow_d, m)
                nc.vector.tensor_scalar(ve[:, :], bank[:, 2, 0:L], 1e-5, None, ALU.add).then_inc(ve_d, 1)

            def normalise(m, r):
                dve.wait_ge(pow_d, m + 1)
                at_least(dve, mm1_d, 3 * (m - 1))
                nc.vector.tensor_tensor(hn[:, r % 2, :], bank[:, r % 2, 0:L], rs[:, :], ALU.mult).then_inc(hn_d, 1)

            def residual(m, r, old):
                dve.wait_ge(mm2_d, m + 1)
                dve.wait_ge(x_in[r % NBUF], 16 * G * (old + 1))
                at_least(dve, x1_out[r % NBUF], 16 * G * old)
                nc.vector.scalar_tensor_tensor(x1o[:, r % NBUF, :], bank[:, 6 + r % 2, 0:L], b2s[:, 0:1],
                                               xt[:, r % NBUF, :], ALU.add, ALU.add).then_inc(x1_dn, 1)

            add_eps(0)
            normalise(0, 0)
            add_eps(1)
            normalise(1, 1)
            for m in range(1, NBUF):
                residual(m - 1, m - 1, 0)
                add_eps(m + 1)
                normalise(m + 1, m + 1)
            with dve.Fori(1, NSTEP // NBUF - 1) as j:
                for r in range(NBUF):
                    residual(NBUF * j + (r - 1), (r - 1) % NBUF, j - (1 if r == 0 else 0))
                    add_eps(NBUF * j + (r + 1))
                    normalise(NBUF * j + (r + 1), r + 1)
            for r in range(NBUF):
                m = NSTEP - NBUF + r
                residual(m - 1, (m - 1) % NBUF, (m - 1) // NBUF)
                if m + 1 < NSTEP:
                    add_eps(m + 1)
                    normalise(m + 1, m + 1)
            residual(NSTEP - 1, NBUF - 1, NSTEP // NBUF - 1)

            def norms(i):
                for u in range(2):
                    dve.wait_ge(s["norm_mm"], 2 * i + (u + 1))
                    at_least(dve, s["rn_done"], i)
                    nc.vector.tensor_scalar(nv[:, u, :], bank[:, 6 + u, 0:L], 1e-24, None, ALU.max
                                            ).then_inc(s["nv_done"], 1)

            def scale_y(i, b):
                dve.wait_ge(s["rn_done"], i + 1)
                nc.vector.tensor_tensor(xa[:, b, :, :].rearrange("p u (w i) -> p u w i", w=WX),
                                        yb[:, b, :, :, :].rearrange("p w u i -> p u w i"),
                                        rn[:, :, :].rearrange("p u (w i) -> p u w i", w=WX), ALU.mult).then_inc(s["xa_done"], 1)

            def make_xb(i, b):
                for u in range(2):
                    dve.wait_ge(s["half_mm"], 2 * i + (u + 1))
                    dve.wait_ge(s["xa_done"], i + 1)
                    at_least(dve, s["xbm_done"], i)
                    nc.vector.scalar_tensor_tensor(xb[:, u, :], xa[:, b, u, :], P("maskc"), bank[:, 6 + u, 0:L],
                                                   ALU.mult, ALU.add).then_inc(s["xb_done"], 1)

            def dist_of(t):
                return bank[:, 2, t * NN:(t + 1) * NN]

            def top8(k):
                for t in range(G):
                    nc.vector.max(t8[:, G * k + t, :], dist_of(t)).then_inc(s["t8_done"], 1)

            def mark8(n, k):
                for t in range(G):
                    nc.vector.match_replace(wsel[:, t, :], t8[:, G * k + t, :], dist_of(t), TAKEN
                                            ).then_inc(s["rep_done"], 1)
                dve.wait_ge(s["rep_done"], G * (n + 1) + 1)
                at_least(dve, s["mt_mm"], n - 1)
                nc.vector.tensor_scalar(msk[:, k, :, :], wsel[:, :, :], TAKEN / 2, None, ALU.is_gt
                                        ).then_inc(s["mask_done"], 1)

            def reduce(n, k, g):
                dve.wait_ge(s["gat_mm"], G * n + (g + 1))
                src = bank[0:2 * O, g % 2, :].rearrange("p (k i) -> p i k", k=NB)
                for h, op in enumerate((ALU.max, ALU.min)):
                    nc.vector.tensor_reduce(red[:, k, h, g, :], src, axis=mybir.AxisListType.X, op=op
                                            ).then_inc(s["red_done"], 1)

            def with_self(n, k):
                dve.wait_ge(s["q_done"], n + 1)
                dve.wait_ge(s["red_done"], 2 * G * (n + 1))
                at_least(dve, s["addq_done"], n)
                for h, op in enumerate((ALU.max, ALU.min)):
                    last = nc.vector.tensor_tensor(red9[:, h, :, :].rearrange("p g i -> p (g i)"),
                                                   red[:, k, h, :, :].rearrange("p g i -> p (g i)"),
                                                   bank[0:2 * O, 5, 0:G * NN], op)
                last.then_inc(s["node_done"], 1)

            def best(n, i, wx, b, first):
                dve.wait_ge(s["geg_done"], n + 1)
                if wx == 0 and not first:
                    dve.wait_ge(s["fc2_mm"], G * (i - 1))
                nc.vector.tensor_tensor(og[:, b, :, :, wx, :],
                                        gg[:, 0, :, :].rearrange("p g (r c) -> p g r c", c=WS),
                                        gg[:, 1, :, :].rearrange("p g (r c) -> p g r c", c=WS), ALU.max
                                        ).then_inc(s["og_done"], 1)

            def make_onehot(n, k):
                dve.wait_ge(s["slot_done"], n + 1)
                at_least(dve, s["gat_mm"], G * (n - 1))
                for t in range(NB):
                    last = nc.vector.tensor_scalar(onehot[:, k, :, t, :], slot[:, k, :, :], float(t + 1 - 99), None,
                                                   ALU.is_equal)
                last.then_inc(s["onehot_done"], 1)

            def final_sum(i, b, old):
                for gp in range(2):
                    dve.wait_ge(s["fc2_mm"], 2 * (2 * i + (gp + 1)))
                    if gp == 0:
                        dve.wait_ge(x1r_in[b], 32 * (old + 1))
                        at_least(dve, final_out[b], 64 * old)
                    nc.vector.scalar_tensor_tensor(outs[:, b, gp, :], bank[:, 6 + gp, 0:L], c2[:, 0:1], x1r[:, b, gp, :],
                                                   ALU.add, ALU.add).then_inc(s["fin_done"], 1)

            def dve_slot(n, i, j, r, gather=True, ahead1=True, ahead2=True, pre=True, post=True, first=False):
                wx, b = r % WX, r // WX
                if gather and not (first and r < 2):
                    best(n - 2, i, (wx - 2) % WX, ((r - 2) % (2 * WX)) // WX, first)
                if gather:
                    reduce(n, r % 2, 0)
                    if not (first and r == 0):
                        with_self(n - 1, (r + 1) % 2)
                    reduce(n, r % 2, 1)
                    reduce(n, r % 2, 2)
                if ahead2:
                    if not gather:
                        dve.wait_ge(s["dist_mm"], n + 3)
                    top8(r % 2)
                    dve.wait_ge(s["t8_done"], G * (n + 3))
                if gather:
                    reduce(n, r % 2, 3)
                if ahead2:
                    mark8(n + 2, r % 2)
                if ahead1:
                    make_onehot(n + 1, (r + 1) % 2)
                if pre and wx == 1:
                    norms(i + 1)
                    scale_y(i + 1, (b + 1) % 2)
                if post and wx == 2:
                    final_sum(i - 1, (b + 1) % 2, j - 1 + b)
                if pre and wx == 3:
                    make_xb(i + 1, (b + 1) % 2)

            norms(0)
            scale_y(0, 0)
            make_xb(0, 0)
            dve_slot(-2, -1, -1, 12, gather=False, ahead1=False, pre=False, post=False)
            dve_slot(-1, -1, -1, 13, gather=False, pre=False, post=False)
            for r in range(2 * WX):
                dve_slot(r, r // WX, 0, r, post=r >= WX + 2, first=True)
            with dve.Fori(1, NI // 2 - 1) as j:
                for r in range(2 * WX):
                    dve_slot(2 * WX * j + r, 2 * j + r // WX, j, r)
            for r in range(2 * WX):
                n = NU - 2 * WX + r
                dve_slot(n, NI - 2 + r // WX, NI // 2 - 1, r, ahead1=n + 1 < NU, ahead2=n + 2 < NU, pre=r < WX)
            with_self(NU - 1, 1)
            for n in (NU - 2, NU - 1):
                best(n, NI - 1, n % WX, 1, False)
            final_sum(NI - 1, 1, NI // 2 - 1)

        @block.tensor
        def _(pe):
            mm = nc.tensor.matmul

            def conv_pair(j, b):
                pe.wait_ge(conv_in[b], 64 * (j + 1))
                at_least(pe, conv_evac_a, 4 * j + (2 * b - 2))
                at_least(pe, conv_evac_v, 4 * j + (2 * b - 2))
                for dw in range(KS):
                    for ch in range(CH):
                        last = mm(bank[0:KC, 4 * b + ch, 0:CL].rearrange("p (b w) -> p b w", w=HW),
                                  toep[b][:, dw, :], xrow[b][:, 8 * ch:8 * ch + 8, dw:dw + HW],
                                  start=dw == 0, stop=dw == KS - 1)
                last.then_inc(conv_mm, 1)

            for b in range(2):
                conv_pair(0, b)
            with pe.Fori(1, CP // 2) as j:
                for b in range(2):
                    conv_pair(j, b)

            pe.wait_ge(par_in, 16)
            pe.wait_ge(conv_evac_v, 2 * CP)
            pe.wait_ge(conv_evac_a, 2 * CP)
            for t in range(3):
                last = mm(bank[:, 6, t:t + 1], P("w1")[:, 128 * t:128 * t + 128], P("ln_b"), start=True, stop=True)
            last.then_inc(lnb_dot, 1)
            pe.wait_ge(ready, 1)
            pe.wait_ge(zeroed, 2)

            def centre(m, r, old):
                pe.wait_ge(h_in[r % NBUF], 16 * G * (old + 1))
                at_least(pe, hn_d, m - 1)
                mm(bank[:, r % 2, 0:L].rearrange("p (h w) -> p h w", w=HW), P("center"),
                   ht[:, r % NBUF, :].rearrange("p (h w) -> p h w", w=HW)[:, ::-1, :], start=True, stop=True).then_inc(ctr_d, 1)

            def variance(m):
                pe.wait_ge(sq_d, m + 1)
                at_least(pe, ve_d, m)
                mm(bank[:, 2, 0:L], P("mean"), sq[:, :], start=True, stop=True).then_inc(var_d, 1)

            def expand(m, r):
                pe.wait_ge(hn_d, m + 1)
                for t in range(3):
                    at_least(pe, gelu_d, 3 * (m - 1) + (t + 1))
                    mm(bank[:, 3 + t, 0:L], w1g[:, t, :], hn[:, r % 2, :], start=True, stop=True).then_inc(mm1_d, 1)

            def contract(m, r):
                at_least(pe, x1_dn, m - 1)
                for t in range(3):
                    pe.wait_ge(gelu_d, 3 * m + (t + 1))
                    last = mm(bank[:, 6 + r % 2, 0:L], w2s[:, t, :], gl[:, t, :], start=t == 0, stop=t == 2)
                last.then_inc(mm2_d, 1)

            centre(0, 0, 0)
            variance(0)
            for m in range(NBUF):
                if m:
                    contract(m - 1, m - 1)
                centre(m + 1, m + 1, (m + 1) // NBUF)
                expand(m, m)
                variance(m + 1)
            with pe.Fori(1, NSTEP // NBUF - 1) as j:
                for r in range(NBUF):
                    contract(NBUF * j + (r - 1), (r - 1) % NBUF)
                    centre(NBUF * j + (r + 1), r + 1, j + (r + 1) // NBUF)
                    expand(NBUF * j + r, r)
                    variance(NBUF * j + (r + 1))
            for m in range(NSTEP - NBUF, NSTEP):
                contract(m - 1, m - 1)
                if m + 1 < NSTEP:
                    centre(m + 1, m + 1, (m + 1) // NBUF)
                expand(m, m)
                if m + 1 < NSTEP:
                    variance(m + 1)
            contract(NSTEP - 1, NSTEP - 1)
            pe.wait_ge(x1_dn, NSTEP)
            pe.wait_ge(zeroed, 3)

            def fc1(i, b, old):
                for u in range(2):
                    if u == 0:
                        pe.wait_ge(x1t_in[b], 64 * (old + 1))
                    at_least(pe, s["xb_done"], 2 * i)
                    mm(bank[:, 6 + u, 0:L].rearrange("p (w r c) -> p w r c", w=WX, c=WS), P("fc1"),
                       x1t[:, b, u, :].rearrange("p (r w c) -> p w r c", w=WX, c=WS), start=True, stop=True).then_inc(s["fc1_mm"], 1)

            def norm(i):
                pe.wait_ge(s["ysq_done"], i + 1)
                for u in range(2):
                    mm(bank[:, 6 + u, 0:L], P("norm"), sq2[:, u, :], start=True, stop=True).then_inc(s["norm_mm"], 1)

            def halfsq(i):
                pe.wait_ge(s["xasq_done"], i + 1)
                at_least(pe, s["fin_done"], 2 * (i - 1))
                for u in range(2):
                    mm(bank[:, 6 + u, 0:L], P("halfsq"), sq2[:, u, :], start=True, stop=True).then_inc(s["half_mm"], 1)

            def fc2(i, b):
                pe.wait_ge(s["og_done"], WX * (i + 1))
                pe.wait_ge(s["nv_done"], 2 * min(i + 3, NI) if isinstance(i, int) else 2 * (i + 3))
                for g in range(G):
                    mm(bank[64 * (g % 2):64 * (g % 2) + 64, 6 + g // 2, 0:L], f2[0:2 * O, :],
                       og[:, b, g, :, :, :].rearrange("p r w c -> p (r w c)"), start=True, stop=True
                       ).then_inc(s["fc2_mm"], 1)

            def dist(n, i, b, wx):
                pe.wait_ge(s["xbm_done"], i + 1)
                at_least(pe, s["rep_done"], G * n + 1 if not isinstance(n, int) or n > 0 else 0)
                mm(bank[:, 2, 0:G * NN], identb[:, :], negb[:, :, :].rearrange("p g i -> p (g i)"), start=True,
                   stop=False, skip_group_check=True)
                for h in range(2):
                    for u in range(2):
                        dst = bank[64 * h:64 * h + 64, 2, 0:G * NN].rearrange("p (g u j) -> p u g j", g=2, u=2)
                        last = mm(dst[:, u, :, :], xa[:, b, u, wx * NN:(wx + 1) * NN], xbm[:, b, u, wx, h:G:2, :],
                                  start=False, stop=True, skip_group_check=True)
                last.then_inc(s["dist_mm"], 1)

            def project(n, i, b, wx):
                pe.wait_ge(s["y_done"], 2 * (i + 1))
                at_least(pe, s["lo_done"], n)
                both = yb[:, b, wx, :, :].rearrange("p u i -> p (u i)")
                mm(bank[:, 3, 0:G * O], both, wp[:, :], start=True, stop=False, skip_group_check=True
                   ).then_inc(s["p_mm"], 1)

            def subtract(n, k, part, waits, done):
                pe.wait_ge(waits, n + 1)
                for u in range(2):
                    last = mm(bank[:, 3, 0:G * O].rearrange("p (g o) -> p g o", g=G), nidentb[:, :],
                              pb[:, k, part, :, u * O:(u + 1) * O], start=False, stop=part == 1 and u == 1,
                              skip_group_check=True)
                last.then_inc(done, 1)

            def transpose(n, k):
                pe.wait_ge(s["mask_done"], n + 1)
                at_least(pe, s["slot_done"], n)
                for gp in range(2):
                    last = mm(bank[:, 4, 128 * gp:128 * gp + 128],
                              msk[:, k, 2 * gp:2 * gp + 2, :].rearrange("p u j -> p (u j)"), identb[:, :],
                              start=True, stop=True)
                last.then_inc(s["mt_mm"], 1)

            def ranks(n):
                pe.wait_ge(s["mts_done"], n + 1)
                mm(bank[:, 4, 256:512], prefb[:, :], mts[:, :], start=True, stop=True).then_inc(s["slot_mm"], 1)

            def gather(n, k, g):
                if g == 0:
                    pe.wait_ge(s["onehot_done"], n + 1)
                    pe.wait_ge(s["lo_done"], n + 1)
                at_least(pe, s["red_done"], 2 * (G * n + (g - 1)))
                for part in range(3):
                    last = mm(bank[0:2 * O, g % 2, :], pb[:, k, part, g, :],
                              onehot[:, k, g, :, :].rearrange("p k i -> p (k i)"), start=part == 0, stop=part == 2)
                last.then_inc(s["gat_mm"], 1)

            def self_and_q(n, k, b, wx):
                at_least(pe, s["node_done"], n)
                at_least(pe, s["q_done"], n)
                for g in range(G):
                    for part in range(3):
                        mm(bank[0:2 * O, 5, g * NN:(g + 1) * NN], pb[:, k, part, g, :], i2b[:, :], start=part == 0,
                           stop=part == 2)
                    for u in range(2):
                        last = mm(bank[0:2 * O, 5, (G + g) * NN:(G + g + 1) * NN], wq[:, g, u, :],
                                  yb[:, b, wx, u, :], start=u == 0, stop=u == 1)
                last.then_inc(s["self_mm"], 1)

            def pe_slot(n, i, j, r, gath=True, ahead1=True, ahead2=True, pre=True, post=True):
                wx, b, k = r % WX, r // WX, r % 2
                r1, r2 = (r + 1) % (2 * WX), (r + 2) % (2 * WX)
                if gath:
                    gather(n, k, 0)
                if ahead1:
                    project(n + 1, i + (wx + 1) // WX, r1 // WX, r1 % WX)
                if gath:
                    gather(n, k, 1)
                if ahead1:
                    subtract(n + 1, 1 - k, 0, s["hi_done"], s["res1_mm"])
                if ahead2:
                    dist(n + 2, i + (wx + 2) // WX, r2 // WX, r2 % WX)
                if gath:
                    gather(n, k, 2)
                if ahead1:
                    transpose(n + 1, 1 - k)
                    subtract(n + 1, 1 - k, 1, s["mid_done"], s["res2_mm"])
                if gath:
                    gather(n, k, 3)
                if ahead1:
                    ranks(n + 1)
                if gath:
                    self_and_q(n, k, b, wx)
                if pre and wx == 0:
                    fc1(i + 1, (b + 1) % 2, j + b)
                if pre and wx == 1:
                    norm(i + 1)
                if post and wx == 2:
                    fc2(i - 1, (b + 1) % 2)
                if pre and wx == 3:
                    halfsq(i + 1)

            fc1(0, 0, 0)
            norm(0)
            halfsq(0)
            pe_slot(-2, -1, -1, 12, gath=False, ahead1=False, pre=False, post=False)
            pe_slot(-1, -1, -1, 13, gath=False, pre=False, post=False)
            for r in range(2 * WX):
                pe_slot(r, r // WX, 0, r, post=r >= WX)
            with pe.Fori(1, NI // 2 - 1) as j:
                for r in range(2 * WX):
                    pe_slot(2 * WX * j + r, 2 * j + r // WX, j, r)
            for r in range(2 * WX):
                n = NU - 2 * WX + r
                pe_slot(n, NI - 2 + r // WX, NI // 2 - 1, r, ahead1=n + 1 < NU, ahead2=n + 2 < NU, pre=r < WX)
            fc2(NI - 1, 1)


def kernel(**inputs):
    import numpy as np
    import concourse.bacc as bacc
    from concourse import mybir as mb
    from concourse.bass_utils import run_bass_kernel_spmd

    a = {k: np.asarray(v) for k, v in inputs.items()}
    par = np.zeros((128, NCOL), np.float32)

    def P(name):
        at, n = COLS[name]
        return par[:, at:at + n]

    for g in range(G):
        r = slice(32 * g, 32 * g + C)
        P("center")[r, r] = np.eye(C) - 1.0 / C
        P("mean")[r, r] = 1.0 / C
        P("norm")[r, r] = 1.0
        P("norm")[32 * g + C, 32 * g + C:32 * g + 32] = 1.0
        P("halfsq")[r, 32 * g + C] = -0.5
        P("maskc")[r] = 1.0
    P("ident")[:] = np.eye(128)
    for u in range(2):
        r = slice(NN * u, NN * u + NN)
        P("prefix")[r, r] = np.triu(np.ones((NN, NN))) - 99.0 * np.eye(NN)
        P("negi")[r] = NEG * np.eye(NN)
        P("i2")[r] = np.eye(NN)
    w1, w2 = a["L0_conv_w1"], a["L0_conv_w2"]
    fc1, ew, fc2 = a["L1_conv_fc1_w"], a["L1_conv_ew"], a["L1_conv_fc2_w"]
    for g in range(G):
        r = slice(32 * g, 32 * g + C)
        P("w1")[r, F * g:F * (g + 1)] = w1
        for f in range(F):
            t, p = divmod(F * g + f, 128)
            P("w2")[p, 128 * t + 32 * g:128 * t + 32 * g + C] = w2[f]
            P("b1")[p, t] = a["L0_conv_b1"][f]
        P("ls_row")[:, r] = a["L0_conv_layer_scale"].reshape(1, C)
        for name, v in (("ln_g", "L0_conv_ln_g"), ("ln_b", "L0_conv_ln_b"), ("b2", "L0_conv_b2"),
                        ("ls", "L0_conv_layer_scale"), ("s1", "L1_conv_fc1_s"), ("b1f", "L1_conv_fc1_b"),
                        ("t1", "L1_conv_fc1_t")):
            P(name)[r, 0] = a[v].reshape(C)
        P("t1")[32 * g + C, 0] = 1.0
        P("fc1")[r, r] = fc1.T
        P("wb")[r, O * g:O * (g + 1)] = ew[:, C:].T
        for u in range(2):
            c = ((g * 2 + u) * 2 + u) * O
            P("wa_q")[r, c:c + O] = ew[:, :C].T
            P("wb_q")[r, c:c + O] = ew[:, C:].T
    P("es_row")[:] = a["L1_conv_es"].reshape(1, O)
    for k in range(2):
        P("conv_b")[k * HW:(k + 1) * HW, :] = a["L0_conv_conv_b"].reshape(CP, 2)[:, k]
        r = slice(O * k, O * (k + 1))
        for name in ("eb", "es", "et"):
            P(name)[r, 0] = a["L1_conv_" + name]
        P("fc2")[r, C * k:C * (k + 1)] = fc2.T
        P("s2_row")[:, C * k:C * (k + 1)] = a["L1_conv_fc2_s"].reshape(1, C)
        for h in range(2):
            r = slice(64 * h + C * k, 64 * h + C * (k + 1))
            for name, v in (("s2", "L1_conv_fc2_s"), ("b2f", "L1_conv_fc2_b"), ("t2", "L1_conv_fc2_t")):
                P(name)[r, 0] = a[v]
    z = np.zeros((C, KS, ZL), np.float32)
    z[:, :, HW - 1 - PAD:HW + PAD] = a["L0_conv_conv_w"].reshape(C, KS, KS).transpose(0, 2, 1)

    nc = bacc.Bacc("TRN2", target_bir_lowering=False, num_devices=1)
    arrays = {"x": np.ascontiguousarray(a["x"]), "zfilt": z, "params": par}
    args = [nc.dram_tensor("in_" + n, v.shape, mb.dt.float32, kind="ExternalInput").ap() for n, v in arrays.items()]
    args.append(nc.dram_tensor("out0", (B, C, HW, HW), mb.dt.float32, kind="ExternalOutput").ap())
    build(nc, *args)
    res = run_bass_kernel_spmd(nc, [{"in_" + n: v for n, v in arrays.items()}], core_ids=[0])
    return res.results[0]["out0"]
```

```python
import concourse.bass as bass
import concourse.mybir as mybir
from contextlib import ExitStack

B, C, HW = 32, 24, 56
F = 4 * C
O = 2 * C
KS = 7
PAD = KS // 2
WS = 8
NN = WS * WS
NB = 8
IMG = HW * HW
CHAN = C * IMG

G = 4
Q = B // (2 * G)
SR = WS
L = SR * HW
NS = HW // SR
NI = Q * NS
NSTEP = 2 * NI
WX = HW // WS
NBLK = 4
LB = L // NBLK
NU = NI * WX
CP = C // 2
ZL = 2 * HW - 1
NEG = -1.0e30
TAKEN = 1.0e30

COLS = {}
_at = 0
for _name, _n in (("center", 128), ("mean4", G), ("norm4", G), ("halfsq", 128), ("ident", 128), ("prefix", 128),
                  ("negi", NN), ("i2", NN), ("maskc", 1),
                  ("w1", G * F), ("w2", 3 * 128), ("ls_row", 128), ("ln_g", 1), ("ln_b", 1), ("b1", 3), ("b2", 1), ("ls", 1),
                  ("conv_b", CP),
                  ("fc1", 128), ("s1", 1), ("b1f", 1), ("t1", 1),
                  ("wb", G * O), ("es_row", O), ("wa_q", G * 4 * O), ("wb_q", G * 4 * O),
                  ("eb", 1), ("es", 1), ("et", 1), ("fc2", 64), ("s2_row", 64), ("s2", 1), ("b2f", 1), ("t2", 1)):
    COLS[_name] = (_at, _n)
    _at += _n
NCOL = _at


def build(nc, x, zfilt, params, out):
    F32, BF = mybir.dt.float32, mybir.dt.bfloat16
    ALU, ACT = mybir.AluOpType, mybir.ActivationFunctionType
    ctx = ExitStack()
    with ctx:
        def sb(name, shape, dt=F32):
            return ctx.enter_context(nc.sbuf_tensor(name, shape, dt))

        def sem(name):
            return ctx.enter_context(nc.semaphore(name))

        def at_least(eng, s, count):
            if isinstance(count, int) and count <= 0:
                return
            eng.wait_ge(s, count)

        conv_d = nc.dram_tensor("conv_d", (C, HW, B, HW), F32, kind="Internal").ap()
        x1_d = nc.dram_tensor("x1_d", (NI, G, 2 * C, L), F32, kind="Internal").ap()

        par = sb("par", [128, NCOL])

        def P(name):
            a, n = COLS[name]
            return par[:, a:a + n]

        KC = 2 * HW
        toep = [sb(f"toep{i}", [KC, KS, KC]) for i in range(2)]
        xrow = [sb(f"xrow{i}", [KC, B, HW + 2 * PAD]) for i in range(2)]
        cvo = [sb(f"cvo{i}", [KC, B * HW]) for i in range(2)]
        NBUF = 4
        ht = sb("ht", [128, NBUF, L])
        xt = sb("xt", [128, NBUF, L])
        x1o = sb("x1o", [128, NBUF, L])
        sq = sb("sq", [128, L])
        hcs = sb("hcs", [128, NBUF, L])
        ve = sb("ve", [LB, NBLK * G])
        rs = sb("rs", [LB, NBLK * G])
        rse = sb("rse", [LB, 2, NBLK, G, 32])
        hn = sb("hn", [128, 2, L])
        gl = sb("gl", [128, 3, L])
        w1g = sb("w1g", [128, 3, 128])
        w2s = sb("w2s", [128, 3, 128])
        b1s = sb("b1s", [128, 3])
        b2s = sb("b2s", [128, 1])
        mhalf = sb("mhalf", [128, WX * G])
        c1 = sb("c1", [128, 1])
        wp = sb("wp", [128, G * O])
        wq = sb("wq", [128, G, 2, 2 * O])
        gb = sb("gb", [128, 1])
        f2 = sb("f2", [128, 64])
        c2 = sb("c2", [128, 1])
        identb = sb("identb", [128, 128], BF)
        nidentb = sb("nidentb", [128, 128], BF)
        prefb = sb("prefb", [128, 128], BF)
        negb = sb("negb", [128, G, NN], BF)
        i2b = sb("i2b", [128, NN], BF)
        x1t = ht[:, :, :].rearrange("p (b u) l -> p b u l", b=2)
        x1r = xt[:, :, :].rearrange("p (b u) l -> p b u l", b=2)
        outs = x1o[:, :, :].rearrange("p (b u) l -> p b u l", b=2)
        yb = sb("yb", [128, 2, WX, 2, NN])
        xa = sb("xa", [128, 2, WX, 2, NN])
        xb = sb("xb", [128, 2 * L])
        xbm = sb("xbm", [128, 2, WX, 2, G, NN])
        sq2 = sb("sq2", [128, 2 * L])
        nv = sb("nv", [128, WX * G])
        rn = sb("rn", [128, WX * G])
        rne = sb("rne", [128, WX, G, 32])
        t8 = sb("t8", [128, 2 * G, NB])
        wsel = sb("wsel", [128, G, NN], BF)
        msk = sb("msk", [128, 2, G, NN], BF)
        mts = sb("mts", [128, G * NN], BF)
        slot = sb("slot", [128, 2, G, NN], BF)
        onehot = sb("onehot", [128, 2, G, NB, NN], BF)
        pb = sb("pb", [128, 2, 3, G, 2 * O], BF)
        red = sb("red", [2 * O, 2, 2, G, NN])
        red9 = sb("red9", [2 * O, 2, G, NN])
        qs = sb("qs", [2 * O, 2, G, NN])
        hq = sb("hq", [2 * O, 2, G, NN])
        gg = sb("gg", [2 * O, 2, G, NN])
        og = sb("og", [2 * O, 2, G, SR, WX, WS])

        bank = ctx.enter_context(nc.psum_tensor("bank", [128, 8, 512], F32))

        par_in, zeroed, mhalf_set, ready, lnb_dot = sem("par_in"), sem("zeroed"), sem("mhalf_set"), sem("ready"), sem("lnb_dot")
        conv_in = [sem(f"conv_in{i}") for i in range(2)]
        conv_mm = sem("conv_mm")
        conv_evac_a, conv_evac_v = sem("conv_evac_a"), sem("conv_evac_v")
        conv_out = [sem(f"conv_out{i}") for i in range(2)]
        h_in = [sem(f"h_in{i}") for i in range(NBUF)]
        x_in = [sem(f"x_in{i}") for i in range(NBUF)]
        x1_out = [sem(f"x1_out{i}") for i in range(NBUF)]
        ctr_d, var_d, mm1_d, mm2_d = sem("ctr_d"), sem("var_d"), sem("mm1_d"), sem("mm2_d")
        sq_d, gelu_d, ve_d, pow_d, hn_d, x1_dn = (sem("sq_d"), sem("gelu_d"), sem("ve_d"), sem("pow_d"), sem("hn_d"),
                                                  sem("x1_dn"))
        hcs_d, rse_d, rb_d = sem("hcs_d"), sem("rse_d"), sem("rb_d")
        s = {}
        for name in ("fc1_mm", "y_done", "ysq_done", "norm_mm", "nv_done", "rn_done", "rne_done", "rn_mm", "xa_done", "xasq_done", "half_mm",
                     "xb_done", "xbm_done", "dist_mm", "p_mm", "hi_done", "res1_mm", "mid_done", "res2_mm", "lo_done", "t8_done",
                     "rep_done", "mask_done", "mt_mm", "mts_done", "slot_mm", "slot_done", "onehot_done", "gat_mm",
                     "red_done", "self_mm", "node_done", "q_done", "addq_done",
                     "geg_done", "og_done", "fc2_mm", "fin_done"):
            s[name] = sem("g_" + name)
        x1t_in = [sem(f"x1t_in{i}") for i in range(2)]
        x1r_in = [sem(f"x1r_in{i}") for i in range(2)]
        final_out = [sem(f"final_out{i}") for i in range(2)]

        CH = 4
        CL = B // CH * HW
        block = ctx.enter_context(nc.Block())

        @block.sync
        def _(sp):
            sp.dma_start(par[:, :], params).then_inc(par_in, 16)
            sp.wait_ge(zeroed, 1)

            def load_pair(cp, b):
                for k in range(2):
                    sp.dma_start(xrow[b][k * HW:(k + 1) * HW, :, PAD:PAD + HW],
                                 x[:, 2 * cp + k, :, :].rearrange("b h w -> h b w")).then_inc(conv_in[b], 16)
                    src = zfilt[2 * cp + k, :, 0:HW]
                    band = bass.AP(tensor=src.tensor, offset=src.offset, ap=[[1, HW], [ZL, KS], [1, HW]])
                    sp.dma_start(toep[b][k * HW:(k + 1) * HW, :, k * HW:(k + 1) * HW], band
                                 ).then_inc(conv_in[b], 16)

            def store_pair(cp, b, n):
                sp.wait_ge(conv_evac_a, 2 * (n + 1))
                sp.wait_ge(conv_evac_v, 2 * (n + 1))
                sp.dma_start(conv_d[bass.ds(2 * cp, 2), :, :, :].rearrange("c h b w -> (c h) (b w)"), cvo[b][:, :]
                             ).then_inc(conv_out[b], 16)

            load_pair(0, 0)
            load_pair(1, 1)
            with sp.Fori(0, CP // 2 - 1) as j:
                for b in range(2):
                    sp.wait_ge(conv_mm, 2 * j + b + 1)
                    load_pair(2 * j + b + 2, b)
                    store_pair(2 * j + b, b, 2 * j + b)
            for b in range(2):
                store_pair(CP - 2 + b, b, CP - 2 + b)
            for b in range(2):
                sp.wait_ge(conv_out[b], 16 * (CP // 2))

            sp.wait_ge(zeroed, 2)

            def load_h(m, r):
                i, u = m // 2, r % 2
                q, st = i // NS, i % NS
                at_least(sp, ctr_d, m - NBUF + 1)
                for g in range(G):
                    sp.dma_start(ht[32 * g:32 * g + C, r, :].rearrange("p (h w) -> p h w", w=HW),
                                 conv_d[:, bass.ds((NS - 1) * SR - SR * st, SR), 8 * q + 2 * g + u, :]
                                 ).then_inc(h_in[r], 16)

            def load_x(m, r):
                i, u = m // 2, r % 2
                q, st = i // NS, i % NS
                at_least(sp, x1_dn, m - NBUF + 1)
                for g in range(G):
                    sp.dma_start(xt[32 * g:32 * g + C, r, :],
                                 x[8 * q + 2 * g + u, :, bass.ts(st, SR), :].rearrange("c h w -> c (h w)")
                                 ).then_inc(x_in[r], 16)

            def store_step(m, r):
                i, u = m // 2, r % 2
                sp.wait_ge(x1_dn, m + 1)
                for g in range(G):
                    sp.dma_start(x1_d[i, g, u * C:(u + 1) * C, :], x1o[32 * g:32 * g + C, r, :]).then_inc(x1_out[r], 16)

            for r in range(NBUF):
                load_h(r, r)
            for r in range(NBUF):
                load_x(r, r)
            for r in range(NBUF):
                load_h(NBUF + r, r)
            with sp.Fori(0, NSTEP // NBUF - 2) as j:
                for r in range(NBUF):
                    store_step(NBUF * j + r, r)
                    load_x(NBUF * j + (NBUF + r), r)
                    load_h(NBUF * j + (2 * NBUF + r), r)
            for r in range(NBUF):
                store_step(NSTEP - 2 * NBUF + r, r)
                load_x(NSTEP - NBUF + r, r)
            for r in range(NBUF):
                store_step(NSTEP - NBUF + r, r)
            for r in range(NBUF):
                sp.wait_ge(x1_out[r], 16 * G * (NSTEP // NBUF))

            def load_iter(i, b):
                at_least(sp, s["fc1_mm"], 2 * (i - 1))
                for g in range(G):
                    sp.dma_start(x1t[32 * g:32 * g + C, b, :, :],
                                 x1_d[i, g, :, :].rearrange("(u c) l -> c u l", u=2)).then_inc(x1t_in[b], 16)

            def load_res(i, b):
                at_least(sp, s["fin_done"], 2 * (i - 1))
                for h in range(2):
                    sp.dma_start(x1r[64 * h:64 * h + 2 * C, b, :, :],
                                 x1_d[i, h:G:2, :, :].rearrange("g p l -> p g l")).then_inc(x1r_in[b], 16)

            def store_iter(i, b):
                q, st = i // NS, i % NS
                sp.wait_ge(s["fin_done"], 2 * (i + 1))
                for h in range(2):
                    for gp in range(2):
                        dst = out[bass.ds(8 * q + 4 * gp + 2 * h, 2), :, bass.ts(st, SR), :]
                        sp.dma_start(dst.rearrange("b c h w -> (b c) (h w)"), outs[64 * h:64 * h + 2 * C, b, gp, :]
                                     ).then_inc(final_out[b], 16)

            for b in range(2):
                load_iter(b, b)
                load_res(b, b)
            with sp.Fori(0, NI // 2 - 1) as j:
                for b in range(2):
                    load_iter(2 * j + (b + 2), b)
                    store_iter(2 * j + b, b)
                    load_res(2 * j + (b + 2), b)
            for b in range(2):
                store_iter(NI - 2 + b, b)
            for b in range(2):
                sp.wait_ge(final_out[b], 64 * (NI // 2))

        @block.gpsimd
        def _(pool):
            for b in range(2):
                nc.gpsimd.memset(toep[b][:, :, :], 0.0)
                last = nc.gpsimd.memset(xrow[b][:, :, :], 0.0)
            last.then_inc(zeroed, 1)
            nc.gpsimd.memset(mhalf[:, :], -0.5).then_inc(mhalf_set, 1)
            nc.gpsimd.memset(rse[:, :, :, :, :], 0.0)
            nc.gpsimd.memset(rne[:, :, :, :], 1.0)
            for t in (ht, xt):
                last = nc.gpsimd.memset(t[:, :, :], 0.0)
            last.then_inc(zeroed, 1)
            nc.gpsimd.memset(xbm[:, :, :, :, :, :], 0.0)
            nc.gpsimd.memset(pb[:, :, :, :, :], 0.0).then_inc(zeroed, 1)
            pool.wait_ge(mhalf_set, 1)

            def inv_std(m):
                pool.wait_ge(ve_d, m + 1)
                at_least(pool, rse_d, m)
                nc.gpsimd.tensor_tensor(rs[:, :], ve[:, :], mhalf[0:LB, 0:NBLK * G], ALU.pow).then_inc(pow_d, 1)

            inv_std(0)
            with pool.Fori(1, NSTEP) as m:
                inv_std(m)

            def inv_norm(i):
                pool.wait_ge(s["nv_done"], i + 1)
                at_least(pool, s["rne_done"], i)
                nc.gpsimd.tensor_tensor(rn[:, :], nv[:, :], mhalf[:, :], ALU.pow).then_inc(s["rn_done"], 1)

            def add_q(n, k):
                pool.wait_ge(s["q_done"], n + 1)
                pool.wait_ge(s["node_done"], n + 1)
                at_least(pool, s["geg_done"], n)
                nc.gpsimd.tensor_tensor(hq[:, :, :, :].rearrange("p h g i -> p h (g i)"),
                                        red9[:, :, :, :].rearrange("p h g i -> p h (g i)"),
                                        qs[:, k, :, :].rearrange("p g i -> p (g i)").unsqueeze(1).broadcast_to(
                                            [2 * O, 2, G * NN]), ALU.add).then_inc(s["addq_done"], 1)

            def pool_slot(n, i, r, add=True, pre=True):
                if add:
                    add_q(n - 1, (r + 1) % 2)
                if pre and r % WX == 1:
                    inv_norm(i + 1)

            inv_norm(0)
            for r in range(2 * WX):
                pool_slot(r, r // WX, r, add=r > 0)
            with pool.Fori(1, NI // 2 - 1) as j:
                for r in range(2 * WX):
                    pool_slot(2 * WX * j + r, 2 * j + r // WX, r)
            for r in range(2 * WX):
                pool_slot(NU - 2 * WX + r, NI - 2 + r // WX, r, pre=r < WX)
            add_q(NU - 1, 1)

        @block.scalar
        def _(act):
            act.wait_ge(par_in, 16)
            with act.Fori(0, CP // 2) as j:
                for b in range(2):
                    act.wait_ge(conv_mm, 2 * j + b + 1)
                    act.wait_ge(conv_out[b], 16 * j)
                    for ch in range(2):
                        nc.scalar.activation(cvo[b][:, ch * CL:(ch + 1) * CL], bank[0:KC, 4 * b + ch, 0:CL], ACT.Identity,
                                             bias=P("conv_b")[0:KC, bass.ds(2 * j + b, 1)], scale=1.0
                                             ).then_inc(conv_evac_a, 1)

            def square(m, r):
                act.wait_ge(ctr_d, m + 1)
                nc.scalar.activation(sq[:, :], bank[:, 0, 0:L], ACT.Square).then_inc(sq_d, 1)
                at_least(act, hn_d, m - NBUF + 1)
                nc.scalar.copy(hcs[:, r % NBUF, :], bank[:, 0, 0:L]).then_inc(hcs_d, 1)

            def gelu(m, r):
                for t in range(3):
                    act.wait_ge(mm1_d, 3 * m + (t + 1))
                    nc.scalar.activation(gl[:, t, :], bank[:, 3 + t, 0:L], ACT.Gelu, bias=b1s[:, t:t + 1], scale=1.0
                                         ).then_inc(gelu_d, 1)

            act.wait_ge(ready, 1)
            act.wait_ge(zeroed, 3)
            for m in range(3):
                square(m, m)
            for m in range(NBUF):
                square(m + 3, m + 3)
                gelu(m, m)
            with act.Fori(1, NSTEP // NBUF - 1) as j:
                for r in range(NBUF):
                    square(NBUF * j + (r + 3), r + 3)
                    gelu(NBUF * j + r, r)
            for m in range(NSTEP - NBUF, NSTEP):
                if m + 3 < NSTEP:
                    square(m + 3, m + 3)
                gelu(m, m)

            def make_y(i, b):
                for u in range(2):
                    act.wait_ge(s["fc1_mm"], 2 * i + (u + 1))
                    nc.scalar.activation(yb[:, b, :, u, :], bank[:, 6 + u, 0:L].rearrange("p (w i) -> p w i", w=WX), ACT.Identity, bias=c1[:, 0:1],
                                         scale=P("s1")).then_inc(s["y_done"], 1)
                act.wait_ge(s["y_done"], 2 * (i + 1))
                nc.scalar.activation(sq2[:, :], yb[:, b, :, :, :].rearrange("p w u i -> p (w u i)"), ACT.Square).then_inc(s["ysq_done"], 1)

            def square_xa(i, b):
                act.wait_ge(s["xa_done"], i + 1)
                nc.scalar.activation(sq2[:, :], xa[:, b, :, :, :].rearrange("p w u i -> p (w u i)"), ACT.Square).then_inc(s["xasq_done"], 1)

            def spread_xb(i, b):
                act.wait_ge(s["xb_done"], 2 * (i + 1))
                at_least(act, s["dist_mm"], WX * (i - 1))
                for g in range(G):
                    last = nc.scalar.copy(xbm[32 * g:32 * g + 32, b, :, :, g, :].rearrange("p w u i -> p (w u) i"),
                                          xb[32 * g:32 * g + 32, :].rearrange("p (v i) -> p v i", i=NN))
                last.then_inc(s["xbm_done"], 1)

            def split(n, k, part, waits, done):
                act.wait_ge(waits, n + 1)
                src = bank[:, 3, 0:G * O].rearrange("p (g o) -> p g o", g=G)
                for u in range(2):
                    last = nc.scalar.copy(pb[64 * u:64 * u + 64, k, part, :, u * O:(u + 1) * O],
                                          src[64 * u:64 * u + 64, :, :])
                last.then_inc(done, 1)

            def act_slot(n, i, r, gather=True, add=True, ahead1=True, pre=True):
                wx, b = r % WX, r // WX
                if ahead1:
                    split(n + 1, (r + 1) % 2, 0, s["p_mm"], s["hi_done"])
                if ahead1:
                    split(n + 1, (r + 1) % 2, 1, s["res1_mm"], s["mid_done"])
                if ahead1:
                    act.wait_ge(s["mt_mm"], n + 2)
                    nc.scalar.copy(mts[:, :], bank[:, 4, 0:G * NN]).then_inc(s["mts_done"], 1)
                    split(n + 1, (r + 1) % 2, 2, s["res2_mm"], s["lo_done"])
                if ahead1:
                    act.wait_ge(s["slot_mm"], n + 2)
                    nc.scalar.copy(slot[:, (r + 1) % 2, :, :].rearrange("p g i -> p (g i)"),
                                   bank[:, 4, G * NN:2 * G * NN]).then_inc(s["slot_done"], 1)
                if gather:
                    act.wait_ge(s["self_mm"], n + 1)
                    at_least(act, s["addq_done"], n - 1)
                    nc.scalar.copy(qs[:, r % 2, :, :].rearrange("p g i -> p (g i)"), bank[0:2 * O, 5, G * NN:2 * G * NN]
                                   ).then_inc(s["q_done"], 1)
                if add:
                    act.wait_ge(s["addq_done"], n)
                    at_least(act, s["og_done"], n - 1)
                    nc.scalar.activation(gg[:, :, :, :], hq[:, :, :, :], ACT.Gelu, bias=gb[0:2 * O, 0:1], scale=1.0
                                         ).then_inc(s["geg_done"], 1)
                if pre and wx == 0:
                    make_y(i + 1, (b + 1) % 2)
                if pre and wx == 3:
                    square_xa(i + 1, (b + 1) % 2)
                if pre and wx == 4:
                    spread_xb(i + 1, (b + 1) % 2)

            make_y(0, 0)
            square_xa(0, 0)
            spread_xb(0, 0)
            act_slot(-1, -1, 13, gather=False, add=False, pre=False)
            for r in range(2 * WX):
                act_slot(r, r // WX, r, add=r > 0)
            with act.Fori(1, NI // 2 - 1) as j:
                for r in range(2 * WX):
                    act_slot(2 * WX * j + r, 2 * j + r // WX, r)
            for r in range(2 * WX):
                n = NU - 2 * WX + r
                act_slot(n, NI - 2 + r // WX, r, ahead1=n + 1 < NU, pre=r < WX)
            act_slot(NU, NI, 0, gather=False, ahead1=False, pre=False)

        @block.vector
        def _(dve):
            dve.wait_ge(par_in, 16)

            with dve.Fori(0, CP // 2) as j:
                for b in range(2):
                    dve.wait_ge(conv_mm, 2 * j + b + 1)
                    dve.wait_ge(conv_out[b], 16 * j)
                    for ch in range(2, 4):
                        nc.vector.tensor_scalar(cvo[b][:, ch * CL:(ch + 1) * CL], bank[0:KC, 4 * b + ch, 0:CL],
                                                P("conv_b")[0:KC, bass.ds(2 * j + b, 1)], None, ALU.add
                                                ).then_inc(conv_evac_v, 1)

            dve.wait_ge(lnb_dot, 1)
            nc.vector.tensor_tensor(b1s[:, :], bank[:, 6, 0:3], P("b1"), ALU.add)
            nc.vector.tensor_scalar(w1g[:, :, :].rearrange("p t m -> p (t m)"), P("w1"), P("ln_g"), None, ALU.mult)
            for t in range(3):
                nc.vector.tensor_tensor(w2s[:, t, :], P("w2")[:, 128 * t:128 * t + 128], P("ls_row"), ALU.mult)
            nc.vector.tensor_tensor(b2s[:, :], P("b2"), P("ls"), ALU.mult)
            nc.vector.scalar_tensor_tensor(c1[:, :], P("b1f"), P("s1"), P("t1"), ALU.mult, ALU.add)
            nc.vector.tensor_tensor(wp[:, :].rearrange("p (g o) -> p g o", g=G), P("wb").rearrange("p (g o) -> p g o", g=G),
                                    P("es_row").unsqueeze(1).broadcast_to([128, G, O]), ALU.mult)
            wqf = wq[:, :, :, :].rearrange("p g u m -> p (g u m)")
            nc.vector.tensor_tensor(wqf, P("wa_q"), P("wb_q"), ALU.subtract).then_inc(s["rep_done"], 1)
            dve.wait_ge(s["rep_done"], 1)
            wqv = wq[:, :, :, :].rearrange("p g u (v o) -> p (g u v) o", v=2)
            nc.vector.tensor_tensor(wqv, wqv, P("es_row").unsqueeze(1).broadcast_to([128, 4 * G, O]), ALU.mult)
            nc.vector.scalar_tensor_tensor(gb[:, :], P("eb"), P("es"), P("et"), ALU.mult, ALU.add)
            nc.vector.tensor_tensor(f2[:, :], P("fc2"), P("s2_row"), ALU.mult)
            nc.vector.scalar_tensor_tensor(c2[:, :], P("b2f"), P("s2"), P("t2"), ALU.mult, ALU.add)
            nc.vector.tensor_copy(identb[:, :], P("ident"))
            nc.vector.tensor_scalar(nidentb[:, :], P("ident"), -1.0, None, ALU.mult)
            nc.vector.tensor_copy(prefb[:, :], P("prefix"))
            nc.vector.tensor_copy(negb[:, :, :], P("negi").unsqueeze(1).broadcast_to([128, G, NN]))
            nc.vector.tensor_copy(i2b[:, :], P("i2")).then_inc(ready, 1)

            dve.wait_ge(ready, 1)
            dve.wait_ge(zeroed, 2)

            def add_eps(m):
                dve.wait_ge(var_d, m + 1)
                at_least(dve, pow_d, m)
                nc.vector.tensor_scalar(ve[:, :], bank[0:LB, 2, 0:NBLK * G], 1e-5, None, ALU.add).then_inc(ve_d, 1)

            def spread_std(m, r):
                dve.wait_ge(pow_d, m + 1)
                at_least(dve, rb_d, m - 1)
                nc.vector.tensor_copy(rse[:, r % 2, :, :, 0:C].rearrange("p k g c -> p (k g) c"),
                                      rs[:, :].unsqueeze(2).broadcast_to([LB, NBLK * G, C])).then_inc(rse_d, 1)

            def normalise(m, r):
                dve.wait_ge(rb_d, m + 1)
                dve.wait_ge(hcs_d, m + 1)
                at_least(dve, mm1_d, 3 * (m - 1))
                nc.vector.tensor_tensor(hn[:, r % 2, :], bank[:, 1, 0:L], hcs[:, r % NBUF, :], ALU.mult
                                        ).then_inc(hn_d, 1)

            def residual(m, r, old):
                dve.wait_ge(mm2_d, m + 1)
                dve.wait_ge(x_in[r % NBUF], 16 * G * (old + 1))
                at_least(dve, x1_out[r % NBUF], 16 * G * old)
                nc.vector.scalar_tensor_tensor(x1o[:, r % NBUF, :], bank[:, 6 + r % 2, 0:L], b2s[:, 0:1],
                                               xt[:, r % NBUF, :], ALU.add, ALU.add).then_inc(x1_dn, 1)

            def mlp_slot(m, r, old, first=False):
                end = NSTEP if isinstance(m, int) else 1 << 30
                now = m if isinstance(m, int) else 0
                if not first:
                    residual(m - 1, (r - 1) % NBUF, old)
                if now + 2 < end:
                    spread_std(m + 2, r)
                if now + 1 < end:
                    normalise(m + 1, r + 1)
                if now + 3 < end:
                    add_eps(m + 3)

            add_eps(0)
            spread_std(0, 0)
            add_eps(1)
            spread_std(1, 1)
            normalise(0, 0)
            add_eps(2)
            for m in range(NBUF):
                mlp_slot(m, m, 0, first=m == 0)
            with dve.Fori(1, NSTEP // NBUF - 1) as j:
                for r in range(NBUF):
                    mlp_slot(NBUF * j + r, r, j - (1 if r == 0 else 0))
            for m in range(NSTEP - NBUF, NSTEP):
                mlp_slot(m, m % NBUF, (m - 1) // NBUF)
            residual(NSTEP - 1, NBUF - 1, NSTEP // NBUF - 1)

            def norms(i):
                dve.wait_ge(s["norm_mm"], i + 1)
                at_least(dve, s["rn_done"], i)
                nc.vector.tensor_scalar(nv[:, :], bank[:, 6, 0:WX * G], 1e-24, None, ALU.max).then_inc(s["nv_done"], 1)

            def spread_norm(i):
                dve.wait_ge(s["rn_done"], i + 1)
                at_least(dve, s["rn_mm"], i)
                nc.vector.tensor_copy(rne[:, :, :, 0:C].rearrange("p w g c -> p (w g) c"),
                                      rn[:, :].unsqueeze(2).broadcast_to([128, WX * G, C])).then_inc(s["rne_done"], 1)

            def scale_y(i, b):
                dve.wait_ge(s["rn_mm"], i + 1)
                for k, (lo, hi) in enumerate(((0, 4), (4, WX))):
                    last = nc.vector.tensor_tensor(xa[:, b, lo:hi, :, :].rearrange("p w u i -> p (w u i)"),
                                                   bank[:, 6 + k, 0:(hi - lo) * 2 * NN],
                                                   yb[:, b, lo:hi, :, :].rearrange("p w u i -> p (w u i)"), ALU.mult)
                last.then_inc(s["xa_done"], 1)

            def make_xb(i, b):
                for u in range(2):
                    dve.wait_ge(s["half_mm"], 2 * i + (u + 1))
                    dve.wait_ge(s["xa_done"], i + 1)
                    at_least(dve, s["xbm_done"], i)
                    nc.vector.scalar_tensor_tensor(xb[:, u * L:(u + 1) * L],
                                                   xa[:, b, :, :, :].rearrange("p w u i -> p (w u i)")[:, u * L:(u + 1) * L],
                                                   P("maskc"), bank[:, 6 + u, 0:L],
                                                   ALU.mult, ALU.add).then_inc(s["xb_done"], 1)

            def dist_of(t):
                return bank[:, 2, t * NN:(t + 1) * NN]

            def top8(k):
                for t in range(G):
                    nc.vector.max(t8[:, G * k + t, :], dist_of(t)).then_inc(s["t8_done"], 1)

            def mark8(n, k):
                for t in range(G):
                    nc.vector.match_replace(wsel[:, t, :], t8[:, G * k + t, :], dist_of(t), TAKEN
                                            ).then_inc(s["rep_done"], 1)
                dve.wait_ge(s["rep_done"], G * (n + 1) + 1)
                at_least(dve, s["mt_mm"], n - 1)
                nc.vector.tensor_scalar(msk[:, k, :, :], wsel[:, :, :], TAKEN / 2, None, ALU.is_gt
                                        ).then_inc(s["mask_done"], 1)

            def reduce(n, k, g):
                dve.wait_ge(s["gat_mm"], G * n + (g + 1))
                src = bank[0:2 * O, g % 2, :].rearrange("p (k i) -> p i k", k=NB)
                for h, op in enumerate((ALU.max, ALU.min)):
                    nc.vector.tensor_reduce(red[:, k, h, g, :], src, axis=mybir.AxisListType.X, op=op
                                            ).then_inc(s["red_done"], 1)

            def with_self(n, k):
                dve.wait_ge(s["q_done"], n + 1)
                dve.wait_ge(s["red_done"], 2 * G * (n + 1))
                at_least(dve, s["addq_done"], n)
                for h, op in enumerate((ALU.max, ALU.min)):
                    last = nc.vector.tensor_tensor(red9[:, h, :, :].rearrange("p g i -> p (g i)"),
                                                   red[:, k, h, :, :].rearrange("p g i -> p (g i)"),
                                                   bank[0:2 * O, 5, 0:G * NN], op)
                last.then_inc(s["node_done"], 1)

            def best(n, i, wx, b, first):
                dve.wait_ge(s["geg_done"], n + 1)
                if wx == 0 and not first:
                    dve.wait_ge(s["fc2_mm"], G * (i - 1))
                nc.vector.tensor_tensor(og[:, b, :, :, wx, :],
                                        gg[:, 0, :, :].rearrange("p g (r c) -> p g r c", c=WS),
                                        gg[:, 1, :, :].rearrange("p g (r c) -> p g r c", c=WS), ALU.max
                                        ).then_inc(s["og_done"], 1)

            def make_onehot(n, k):
                dve.wait_ge(s["slot_done"], n + 1)
                at_least(dve, s["gat_mm"], G * (n - 1))
                for t in range(NB):
                    last = nc.vector.tensor_scalar(onehot[:, k, :, t, :], slot[:, k, :, :], float(t + 1 - 99), None,
                                                   ALU.is_equal)
                last.then_inc(s["onehot_done"], 1)

            def final_sum(i, b, old):
                for gp in range(2):
                    dve.wait_ge(s["fc2_mm"], 2 * (2 * i + (gp + 1)))
                    if gp == 0:
                        dve.wait_ge(x1r_in[b], 32 * (old + 1))
                        at_least(dve, final_out[b], 64 * old)
                    nc.vector.scalar_tensor_tensor(outs[:, b, gp, :], bank[:, 6 + gp, 0:L], c2[:, 0:1], x1r[:, b, gp, :],
                                                   ALU.add, ALU.add).then_inc(s["fin_done"], 1)

            def dve_slot(n, i, j, r, gather=True, ahead1=True, ahead2=True, pre=True, post=True, first=False):
                wx, b = r % WX, r // WX
                if gather and not (first and r < 2):
                    best(n - 2, i, (wx - 2) % WX, ((r - 2) % (2 * WX)) // WX, first)
                if gather:
                    reduce(n, r % 2, 0)
                    if not (first and r == 0):
                        with_self(n - 1, (r + 1) % 2)
                    reduce(n, r % 2, 1)
                    reduce(n, r % 2, 2)
                if ahead2:
                    if not gather:
                        dve.wait_ge(s["dist_mm"], n + 3)
                    top8(r % 2)
                    dve.wait_ge(s["t8_done"], G * (n + 3))
                if gather:
                    reduce(n, r % 2, 3)
                if ahead2:
                    mark8(n + 2, r % 2)
                if ahead1:
                    make_onehot(n + 1, (r + 1) % 2)
                if pre and wx == 1:
                    norms(i + 1)
                if post and wx == 2:
                    final_sum(i - 1, (b + 1) % 2, j - 1 + b)
                if pre and wx == 2:
                    spread_norm(i + 1)
                if pre and wx == 3:
                    scale_y(i + 1, (b + 1) % 2)
                if pre and wx == 4:
                    make_xb(i + 1, (b + 1) % 2)

            norms(0)
            spread_norm(0)
            scale_y(0, 0)
            make_xb(0, 0)
            dve_slot(-2, -1, -1, 12, gather=False, ahead1=False, pre=False, post=False)
            dve_slot(-1, -1, -1, 13, gather=False, pre=False, post=False)
            for r in range(2 * WX):
                dve_slot(r, r // WX, 0, r, post=r >= WX + 2, first=True)
            with dve.Fori(1, NI // 2 - 1) as j:
                for r in range(2 * WX):
                    dve_slot(2 * WX * j + r, 2 * j + r // WX, j, r)
            for r in range(2 * WX):
                n = NU - 2 * WX + r
                dve_slot(n, NI - 2 + r // WX, NI // 2 - 1, r, ahead1=n + 1 < NU, ahead2=n + 2 < NU, pre=r < WX)
            with_self(NU - 1, 1)
            for n in (NU - 2, NU - 1):
                best(n, NI - 1, n % WX, 1, False)
            final_sum(NI - 1, 1, NI // 2 - 1)

        @block.tensor
        def _(pe):
            mm = nc.tensor.matmul

            def conv_pair(j, b):
                pe.wait_ge(conv_in[b], 64 * (j + 1))
                at_least(pe, conv_evac_a, 4 * j + (2 * b - 2))
                at_least(pe, conv_evac_v, 4 * j + (2 * b - 2))
                for dw in range(KS):
                    for ch in range(CH):
                        last = mm(bank[0:KC, 4 * b + ch, 0:CL].rearrange("p (b w) -> p b w", w=HW),
                                  toep[b][:, dw, :], xrow[b][:, 8 * ch:8 * ch + 8, dw:dw + HW],
                                  start=dw == 0, stop=dw == KS - 1)
                last.then_inc(conv_mm, 1)

            for b in range(2):
                conv_pair(0, b)
            with pe.Fori(1, CP // 2) as j:
                for b in range(2):
                    conv_pair(j, b)

            pe.wait_ge(par_in, 16)
            pe.wait_ge(conv_evac_v, 2 * CP)
            pe.wait_ge(conv_evac_a, 2 * CP)
            for t in range(3):
                last = mm(bank[:, 6, t:t + 1], P("w1")[:, 128 * t:128 * t + 128], P("ln_b"), start=True, stop=True)
            last.then_inc(lnb_dot, 1)
            pe.wait_ge(ready, 1)
            pe.wait_ge(zeroed, 2)

            def centre(m, r, old):
                pe.wait_ge(h_in[r % NBUF], 16 * G * (old + 1))
                at_least(pe, hcs_d, m)
                mm(bank[:, 0, 0:L].rearrange("p (h w) -> p h w", w=HW), P("center"),
                   ht[:, r % NBUF, :].rearrange("p (h w) -> p h w", w=HW)[:, ::-1, :], start=True, stop=True
                   ).then_inc(ctr_d, 1)

            def variance(m):
                pe.wait_ge(sq_d, m + 1)
                at_least(pe, ve_d, m)
                for k in range(NBLK):
                    last = mm(bank[0:LB, 2, G * k:G * k + G], sq[:, LB * k:LB * k + LB], P("mean4"), start=True, stop=True)
                last.then_inc(var_d, 1)

            def turn_std(m, r):
                pe.wait_ge(rse_d, m + 1)
                at_least(pe, hn_d, m)
                for k in range(NBLK):
                    last = mm(bank[:, 1, LB * k:LB * k + LB], rse[:, r % 2, k, :, :].rearrange("p g c -> p (g c)"),
                              P("ident")[0:LB, 0:LB], start=True, stop=True)
                last.then_inc(rb_d, 1)

            def expand(m, r):
                pe.wait_ge(hn_d, m + 1)
                for t in range(3):
                    at_least(pe, gelu_d, 3 * (m - 1) + (t + 1))
                    mm(bank[:, 3 + t, 0:L], w1g[:, t, :], hn[:, r % 2, :], start=True, stop=True).then_inc(mm1_d, 1)

            def contract(m, r):
                at_least(pe, x1_dn, m - 1)
                for t in range(3):
                    pe.wait_ge(gelu_d, 3 * m + (t + 1))
                    last = mm(bank[:, 6 + r % 2, 0:L], w2s[:, t, :], gl[:, t, :], start=t == 0, stop=t == 2)
                last.then_inc(mm2_d, 1)

            def mlp_slot(m, r, j, first=False):
                end = NSTEP if isinstance(m, int) else 1 << 30
                now = m if isinstance(m, int) else 0
                if not first:
                    contract(m - 1, r - 1)
                if now + 3 < end:
                    centre(m + 3, r + 3, j + (r + 3) // NBUF)
                expand(m, r)
                if now + 1 < end:
                    turn_std(m + 1, r + 1)
                if now + 3 < end:
                    variance(m + 3)

            for m in range(3):
                centre(m, m, 0)
                variance(m)
            turn_std(0, 0)
            for m in range(NBUF):
                mlp_slot(m, m, 0, first=m == 0)
            with pe.Fori(1, NSTEP // NBUF - 1) as j:
                for r in range(NBUF):
                    mlp_slot(NBUF * j + r, r, j)
            for r in range(NBUF):
                mlp_slot(NSTEP - NBUF + r, r, NSTEP // NBUF - 1)
            contract(NSTEP - 1, NSTEP - 1)
            pe.wait_ge(x1_dn, NSTEP)
            pe.wait_ge(zeroed, 3)

            def fc1(i, b, old):
                for u in range(2):
                    if u == 0:
                        pe.wait_ge(x1t_in[b], 64 * (old + 1))
                    at_least(pe, s["xb_done"], 2 * i)
                    mm(bank[:, 6 + u, 0:L].rearrange("p (w r c) -> p w r c", w=WX, c=WS), P("fc1"),
                       x1t[:, b, u, :].rearrange("p (r w c) -> p w r c", w=WX, c=WS), start=True, stop=True).then_inc(s["fc1_mm"], 1)

            def norm(i):
                pe.wait_ge(s["ysq_done"], i + 1)
                for w in range(WX):
                    last = mm(bank[:, 6, G * w:G * w + G], sq2[:, 128 * w:128 * w + 128], P("norm4"), start=True, stop=True)
                last.then_inc(s["norm_mm"], 1)

            def turn_norm(i):
                pe.wait_ge(s["rne_done"], i + 1)
                at_least(pe, s["fin_done"], 2 * (i - 1))
                for w in range(WX):
                    last = mm(bank[:, 6 + w // 4, 128 * (w % 4):128 * (w % 4) + 128],
                              rne[:, w, :, :].rearrange("p g c -> p (g c)"), P("ident"), start=True, stop=True)
                last.then_inc(s["rn_mm"], 1)

            def halfsq(i):
                pe.wait_ge(s["xasq_done"], i + 1)
                for u in range(2):
                    mm(bank[:, 6 + u, 0:L], P("halfsq"), sq2[:, L * u:L * u + L], start=True, stop=True
                       ).then_inc(s["half_mm"], 1)

            def fc2(i, b):
                pe.wait_ge(s["og_done"], WX * (i + 1))
                pe.wait_ge(s["nv_done"], min(i + 3, NI) if isinstance(i, int) else i + 3)
                for g in range(G):
                    mm(bank[64 * (g % 2):64 * (g % 2) + 64, 6 + g // 2, 0:L], f2[0:2 * O, :],
                       og[:, b, g, :, :, :].rearrange("p r w c -> p (r w c)"), start=True, stop=True
                       ).then_inc(s["fc2_mm"], 1)

            def dist(n, i, b, wx):
                pe.wait_ge(s["xbm_done"], i + 1)
                at_least(pe, s["rep_done"], G * n + 1 if not isinstance(n, int) or n > 0 else 0)
                mm(bank[:, 2, 0:G * NN], identb[:, :], negb[:, :, :].rearrange("p g i -> p (g i)"), start=True,
                   stop=False, skip_group_check=True)
                for h in range(2):
                    for u in range(2):
                        dst = bank[64 * h:64 * h + 64, 2, 0:G * NN].rearrange("p (g u j) -> p u g j", g=2, u=2)
                        last = mm(dst[:, u, :, :], xa[:, b, wx, u, :], xbm[:, b, wx, u, h:G:2, :],
                                  start=False, stop=True, skip_group_check=True)
                last.then_inc(s["dist_mm"], 1)

            def project(n, i, b, wx):
                pe.wait_ge(s["y_done"], 2 * (i + 1))
                at_least(pe, s["lo_done"], n)
                both = yb[:, b, wx, :, :].rearrange("p u i -> p (u i)")
                mm(bank[:, 3, 0:G * O], both, wp[:, :], start=True, stop=False, skip_group_check=True
                   ).then_inc(s["p_mm"], 1)

            def subtract(n, k, part, waits, done):
                pe.wait_ge(waits, n + 1)
                for u in range(2):
                    last = mm(bank[:, 3, 0:G * O].rearrange("p (g o) -> p g o", g=G), nidentb[:, :],
                              pb[:, k, part, :, u * O:(u + 1) * O], start=False, stop=part == 1 and u == 1,
                              skip_group_check=True)
                last.then_inc(done, 1)

            def transpose(n, k):
                pe.wait_ge(s["mask_done"], n + 1)
                at_least(pe, s["slot_done"], n)
                for gp in range(2):
                    last = mm(bank[:, 4, 128 * gp:128 * gp + 128],
                              msk[:, k, 2 * gp:2 * gp + 2, :].rearrange("p u j -> p (u j)"), identb[:, :],
                              start=True, stop=True)
                last.then_inc(s["mt_mm"], 1)

            def ranks(n):
                pe.wait_ge(s["mts_done"], n + 1)
                mm(bank[:, 4, 256:512], prefb[:, :], mts[:, :], start=True, stop=True).then_inc(s["slot_mm"], 1)

            def gather(n, k, g):
                if g == 0:
                    pe.wait_ge(s["onehot_done"], n + 1)
                    pe.wait_ge(s["lo_done"], n + 1)
                at_least(pe, s["red_done"], 2 * (G * n + (g - 1)))
                for part in range(3):
                    last = mm(bank[0:2 * O, g % 2, :], pb[:, k, part, g, :],
                              onehot[:, k, g, :, :].rearrange("p k i -> p (k i)"), start=part == 0, stop=part == 2)
                last.then_inc(s["gat_mm"], 1)

            def self_and_q(n, k, b, wx):
                at_least(pe, s["node_done"], n)
                at_least(pe, s["q_done"], n)
                for g in range(G):
                    for part in range(3):
                        mm(bank[0:2 * O, 5, g * NN:(g + 1) * NN], pb[:, k, part, g, :], i2b[:, :], start=part == 0,
                           stop=part == 2)
                    for u in range(2):
                        last = mm(bank[0:2 * O, 5, (G + g) * NN:(G + g + 1) * NN], wq[:, g, u, :],
                                  yb[:, b, wx, u, :], start=u == 0, stop=u == 1)
                last.then_inc(s["self_mm"], 1)

            def pe_slot(n, i, j, r, gath=True, ahead1=True, ahead2=True, pre=True, post=True):
                wx, b, k = r % WX, r // WX, r % 2
                r1, r2 = (r + 1) % (2 * WX), (r + 2) % (2 * WX)
                if gath:
                    gather(n, k, 0)
                if ahead1:
                    project(n + 1, i + (wx + 1) // WX, r1 // WX, r1 % WX)
                if gath:
                    gather(n, k, 1)
                if ahead1:
                    subtract(n + 1, 1 - k, 0, s["hi_done"], s["res1_mm"])
                if ahead2:
                    dist(n + 2, i + (wx + 2) // WX, r2 // WX, r2 % WX)
                if gath:
                    gather(n, k, 2)
                if ahead1:
                    transpose(n + 1, 1 - k)
                    subtract(n + 1, 1 - k, 1, s["mid_done"], s["res2_mm"])
                if gath:
                    gather(n, k, 3)
                if ahead1:
                    ranks(n + 1)
                if gath:
                    self_and_q(n, k, b, wx)
                if pre and wx == 0:
                    fc1(i + 1, (b + 1) % 2, j + b)
                if pre and wx == 1:
                    norm(i + 1)
                if post and wx == 2:
                    fc2(i - 1, (b + 1) % 2)
                if pre and wx == 3:
                    turn_norm(i + 1)
                if pre and wx == 4:
                    halfsq(i + 1)

            fc1(0, 0, 0)
            norm(0)
            turn_norm(0)
            halfsq(0)
            pe_slot(-2, -1, -1, 12, gath=False, ahead1=False, pre=False, post=False)
            pe_slot(-1, -1, -1, 13, gath=False, pre=False, post=False)
            for r in range(2 * WX):
                pe_slot(r, r // WX, 0, r, post=r >= WX)
            with pe.Fori(1, NI // 2 - 1) as j:
                for r in range(2 * WX):
                    pe_slot(2 * WX * j + r, 2 * j + r // WX, j, r)
            for r in range(2 * WX):
                n = NU - 2 * WX + r
                pe_slot(n, NI - 2 + r // WX, NI // 2 - 1, r, ahead1=n + 1 < NU, ahead2=n + 2 < NU, pre=r < WX)
            fc2(NI - 1, 1)


def kernel(**inputs):
    import numpy as np
    import concourse.bacc as bacc
    from concourse import mybir as mb
    from concourse.bass_utils import run_bass_kernel_spmd

    a = {k: np.asarray(v) for k, v in inputs.items()}
    par = np.zeros((128, NCOL), np.float32)

    def P(name):
        at, n = COLS[name]
        return par[:, at:at + n]

    for g in range(G):
        r = slice(32 * g, 32 * g + C)
        P("center")[r, r] = np.eye(C) - 1.0 / C
        P("mean4")[r, g] = 1.0 / C
        P("norm4")[r, g] = 1.0
        P("halfsq")[r, 32 * g + C] = -0.5
        P("maskc")[r] = 1.0
    P("ident")[:] = np.eye(128)
    for u in range(2):
        r = slice(NN * u, NN * u + NN)
        P("prefix")[r, r] = np.triu(np.ones((NN, NN))) - 99.0 * np.eye(NN)
        P("negi")[r] = NEG * np.eye(NN)
        P("i2")[r] = np.eye(NN)
    w1, w2 = a["L0_conv_w1"], a["L0_conv_w2"]
    fc1, ew, fc2 = a["L1_conv_fc1_w"], a["L1_conv_ew"], a["L1_conv_fc2_w"]
    for g in range(G):
        r = slice(32 * g, 32 * g + C)
        P("w1")[r, F * g:F * (g + 1)] = w1
        for f in range(F):
            t, p = divmod(F * g + f, 128)
            P("w2")[p, 128 * t + 32 * g:128 * t + 32 * g + C] = w2[f]
            P("b1")[p, t] = a["L0_conv_b1"][f]
        P("ls_row")[:, r] = a["L0_conv_layer_scale"].reshape(1, C)
        for name, v in (("ln_g", "L0_conv_ln_g"), ("ln_b", "L0_conv_ln_b"), ("b2", "L0_conv_b2"),
                        ("ls", "L0_conv_layer_scale"), ("s1", "L1_conv_fc1_s"), ("b1f", "L1_conv_fc1_b"),
                        ("t1", "L1_conv_fc1_t")):
            P(name)[r, 0] = a[v].reshape(C)
        P("t1")[32 * g + C, 0] = 1.0
        P("fc1")[r, r] = fc1.T
        P("wb")[r, O * g:O * (g + 1)] = ew[:, C:].T
        for u in range(2):
            c = ((g * 2 + u) * 2 + u) * O
            P("wa_q")[r, c:c + O] = ew[:, :C].T
            P("wb_q")[r, c:c + O] = ew[:, C:].T
    P("es_row")[:] = a["L1_conv_es"].reshape(1, O)
    for k in range(2):
        P("conv_b")[k * HW:(k + 1) * HW, :] = a["L0_conv_conv_b"].reshape(CP, 2)[:, k]
        r = slice(O * k, O * (k + 1))
        for name in ("eb", "es", "et"):
            P(name)[r, 0] = a["L1_conv_" + name]
        P("fc2")[r, C * k:C * (k + 1)] = fc2.T
        P("s2_row")[:, C * k:C * (k + 1)] = a["L1_conv_fc2_s"].reshape(1, C)
        for h in range(2):
            r = slice(64 * h + C * k, 64 * h + C * (k + 1))
            for name, v in (("s2", "L1_conv_fc2_s"), ("b2f", "L1_conv_fc2_b"), ("t2", "L1_conv_fc2_t")):
                P(name)[r, 0] = a[v]
    z = np.zeros((C, KS, ZL), np.float32)
    z[:, :, HW - 1 - PAD:HW + PAD] = a["L0_conv_conv_w"].reshape(C, KS, KS).transpose(0, 2, 1)

    nc = bacc.Bacc("TRN2", target_bir_lowering=False, num_devices=1)
    arrays = {"x": np.ascontiguousarray(a["x"]), "zfilt": z, "params": par}
    args = [nc.dram_tensor("in_" + n, v.shape, mb.dt.float32, kind="ExternalInput").ap() for n, v in arrays.items()]
    args.append(nc.dram_tensor("out0", (B, C, HW, HW), mb.dt.float32, kind="ExternalOutput").ap())
    build(nc, *args)
    res = run_bass_kernel_spmd(nc, [{"in_" + n: v for n, v in arrays.items()}], core_ids=[0])
    return res.results[0]["out0"]
```

```python
import concourse.bass as bass
import concourse.mybir as mybir
from contextlib import ExitStack

B, C, HW = 32, 24, 56
F = 4 * C
O = 2 * C
KS = 7
PAD = KS // 2
WS = 8
NN = WS * WS
NB = 8
NBP = 3
IMG = HW * HW
CHAN = C * IMG

G = 4
Q = B // (2 * G)
SR = WS
L = SR * HW
NS = HW // SR
NI = Q * NS
NSTEP = 2 * NI
WX = HW // WS
NBLK = 4
LB = L // NBLK
NU = NI * WX
W2 = HW // 2
NSH = (KS + 1) // 2
NCB = 4
ICH = B // 2
KC = 64 + HW
ZL = 2 * HW - 1
NEG = -16384.0
TAKEN = 2.0 ** 100

COLS = {}
_at = 0
for _name, _n in (("center", 128), ("mean4", G), ("norm4", G), ("halfsq", 128), ("chan", 128), ("ident", 128), ("prefix", 128),
                  ("negi", NN), ("i2", NN),
                  ("w1", G * F), ("w2", 3 * 128), ("ls_row", 128), ("ln_g", 1), ("ln_b", 1), ("b1", 3), ("b2", 1), ("ls", 1),
                  ("conv_b", C),
                  ("fc1", 128), ("s1", 1), ("b1f", 1), ("t1", 1),
                  ("wb", G * O), ("es_row", O), ("wa_q", G * 4 * O), ("wb_q", G * 4 * O),
                  ("eb", 1), ("es", 1), ("et", 1), ("fc2", 64), ("s2_row", 64), ("s2", 1), ("b2f", 1), ("t2", 1)):
    COLS[_name] = (_at, _n)
    _at += _n
NCOL = _at


def build(nc, x, zfilt, params, out):
    F32, BF = mybir.dt.float32, mybir.dt.bfloat16
    ALU, ACT = mybir.AluOpType, mybir.ActivationFunctionType
    ctx = ExitStack()
    with ctx:
        def sb(name, shape, dt=F32):
            return ctx.enter_context(nc.sbuf_tensor(name, shape, dt))

        def sem(name):
            return ctx.enter_context(nc.semaphore(name))

        def at_least(eng, s, count):
            if isinstance(count, int) and count <= 0:
                return
            eng.wait_ge(s, count)

        conv_d = nc.dram_tensor("conv_d", (C, 2, HW, B, W2), F32, kind="Internal").ap()
        x1_d = nc.dram_tensor("x1_d", (NI, G, 2 * C, L), F32, kind="Internal").ap()

        par = sb("par", [128, NCOL])

        def P(name):
            a, n = COLS[name]
            return par[:, a:a + n]

        toep = [sb(f"toep{i}", [KC, NSH, KC]) for i in range(NCB)]
        xrow = [sb(f"xrow{i}", [KC, B, HW + 2 * PAD]) for i in range(NCB)]
        NBUF = 4
        ht = sb("ht", [128, NBUF, L])
        xt = sb("xt", [128, NBUF, L])
        x1o = sb("x1o", [128, NBUF, L])
        sq = sb("sq", [128, L])
        hcs = sb("hcs", [128, NBUF, L])
        ve = sb("ve", [LB, NBLK * G])
        rs = sb("rs", [LB, NBLK * G])
        rse = sb("rse", [LB, 2, NBLK, G, 32])
        cvo = [t[0:KC, 2 * i:2 * i + 2, :].rearrange("p a l -> p (a l)") for t in (x1o, hcs) for i in range(2)]
        hn = sb("hn", [128, 2, L])
        gl = sb("gl", [128, 3, L])
        w1g = sb("w1g", [128, 3, 128])
        w2s = sb("w2s", [128, 3, 128])
        b1s = sb("b1s", [128, 3])
        b2s = sb("b2s", [128, 1])
        mhalf = sb("mhalf", [128, WX * G])
        c1 = sb("c1", [128, 1])
        wp = sb("wp", [128, G * O])
        wq = sb("wq", [128, G, 2, 2 * O])
        gb = sb("gb", [128, 1])
        f2 = sb("f2", [128, 64])
        c2 = sb("c2", [128, 1])
        identb = sb("identb", [128, 128], BF)
        nidentb = sb("nidentb", [128, 128], BF)
        unmark = sb("unmark", [128, 128], BF)
        prefb = sb("prefb", [128, 128], BF)
        negb = sb("negb", [128, G, NN], BF)
        i2b = sb("i2b", [128, NN], BF)
        x1t = ht[:, :, :].rearrange("p (b u) l -> p b u l", b=2)
        x1r = xt[:, :, :].rearrange("p (b u) l -> p b u l", b=2)
        outs = x1o[:, :, :].rearrange("p (b u) l -> p b u l", b=2)
        yb = sb("yb", [128, 2, WX, 2, NN])
        xa = sb("xa", [128, 2, WX, 2, NN])
        rnt = sb("rnt", [128, WX, 2, NN])
        xb = sb("xb", [128, 2, WX, 2, NN])
        xam = sb("xam", [128, 2, WX, 2, G, NN])
        sq2 = sb("sq2", [128, 2 * L])
        nv = sb("nv", [128, WX * G])
        rn = sb("rn", [128, WX * G])
        rne = sb("rne", [128, WX, G, 32])
        t8 = sb("t8", [128, 2 * G, NB])
        marked = sb("marked", [128, 2, G, NN], BF)
        mts = sb("mts", [128, G * NN], BF)
        slot = sb("slot", [128, 2, G, NN], BF)
        onehot = sb("onehot", [128, 2, G, NB, NN], BF)
        pb = sb("pb", [128, 2, 3, G, 2 * O], BF)
        red = sb("red", [2 * O, 2, 2, G, NN])
        red9 = sb("red9", [2 * O, 2, G, NN])
        qs = sb("qs", [2 * O, 2, G, NN])
        hq = sb("hq", [2 * O, 2, G, NN])
        gg = sb("gg", [2 * O, 2, G, NN])
        og = sb("og", [2 * O, 2, G, SR, WX, WS])

        bank = ctx.enter_context(nc.psum_tensor("bank", [128, 8, 512], F32))

        par_in, zeroed, mhalf_set = sem("par_in"), sem("zeroed"), sem("mhalf_set")
        ready, lnb_dot, wq_set = sem("ready"), sem("lnb_dot"), sem("wq_set")
        conv_in = [sem(f"conv_in{i}") for i in range(NCB)]
        conv_dup, conv_zeroed, toep_zeroed = sem("conv_dup"), sem("conv_zeroed"), sem("toep_zeroed")
        conv_mm = sem("conv_mm")
        conv_evac_a, conv_evac_v = sem("conv_evac_a"), sem("conv_evac_v")
        conv_out = [sem(f"conv_out{i}") for i in range(NCB)]
        h_in = [sem(f"h_in{i}") for i in range(2)]
        x_in = [sem(f"x_in{i}") for i in range(2)]
        x1_out = [sem(f"x1_out{i}") for i in range(2)]
        ctr_d, var_d, mm1_d, mm2_d = sem("ctr_d"), sem("var_d"), sem("mm1_d"), sem("mm2_d")
        sq_d, gelu_d, ve_d, pow_d, hn_d, x1_dn = (sem("sq_d"), sem("gelu_d"), sem("ve_d"), sem("pow_d"), sem("hn_d"),
                                                  sem("x1_dn"))
        hcs_d, rse_d, rb_d = sem("hcs_d"), sem("rse_d"), sem("rb_d")
        s = {}
        for name in ("fc1_mm", "y_done", "ysq_done", "norm_mm", "nv_done", "rn_done", "rne_done", "rn_mm", "rnt_done", "xa_done", "xasq_done",
                     "half_mm", "xb_done", "xam_done", "dist_mm", "p_mm", "hi_done", "res1_mm", "mid_done", "res2_mm", "lo_done", "t8_done",
                     "mark_done", "mt_mm", "mts_done", "slot_mm", "slot_done", "onehot_done", "onehot_pool", "gat_mm",
                     "red_done", "self_mm", "node_done", "q_done", "addq_done",
                     "geg_done", "og_done", "fc2_mm", "fc2_out", "fin_done"):
            s[name] = sem("g_" + name)
        x1t_in = [sem(f"x1t_in{i}") for i in range(2)]
        x1r_in = [sem(f"x1r_in{i}") for i in range(2)]
        final_out = [sem(f"final_out{i}") for i in range(2)]

        CL = ICH * W2
        EARLY = (0, 2)
        block = ctx.enter_context(nc.Block())

        @block.sync
        def _(sp):

            def load_channel(c, b):
                sp.dma_start(xrow[b][0:HW, :, PAD:PAD + HW], x[:, c, :, :].rearrange("b h w -> h b w")
                             ).then_inc(conv_in[b], 16)
                for pi, po, s0, kx0 in ((0, 0, 0, 0), (1, 1, 0, 0), (1, 0, 0, 1), (0, 1, 1, 1)):
                    src = zfilt[c, kx0:KS, 0:HW]
                    n = (KS - kx0 + 1) // 2
                    band = bass.AP(tensor=src.tensor, offset=src.offset, ap=[[1, HW], [2 * ZL, n], [1, HW]])
                    sp.dma_start(toep[b][64 * pi:64 * pi + HW, s0:s0 + n, 64 * po:64 * po + HW], band
                                 ).then_inc(conv_in[b], 16)

            def store_channel(c, b):
                sp.wait_ge(conv_evac_a, c + 1)
                sp.wait_ge(conv_evac_v, c + 1)
                for p in range(2):
                    sp.dma_start(conv_d[c, p, :, :, :].rearrange("h b v -> h (b v)"), cvo[b][64 * p:64 * p + HW, :]
                                 ).then_inc(conv_out[b], 16)

            for b in range(NCB):
                sp.wait_ge(conv_zeroed, b + 1)
                sp.wait_ge(toep_zeroed, b + 1)
                load_channel(b, b)
                if b == 1:
                    sp.dma_start(par[:, :], params).then_inc(par_in, 16)
            with sp.Fori(0, C // NCB - 1) as j:
                for b in range(NCB):
                    sp.wait_ge(conv_mm, NCB * j + (b + 1))
                    load_channel(NCB * j + (NCB + b), b)
                    store_channel(NCB * j + b, b)
            for b in range(NCB):
                store_channel(C - NCB + b, b)
            for b in range(NCB):
                sp.wait_ge(conv_out[b], 32 * (C // NCB))

            sp.wait_ge(zeroed, 1)

            def load_h(i, b):
                q, st = i // NS, i % NS
                at_least(sp, ctr_d, 2 * (i - 1))
                for g in range(G):
                    sp.dma_start(ht[32 * g:32 * g + C, 2 * b:2 * b + 2, :].rearrange("c a l -> c (a l)").rearrange(
                                     "c (p h w) -> c p h w", p=2, w=2 * W2),
                                 conv_d[:, :, bass.ds((NS - 1) * SR - SR * st, SR), bass.ds(8 * q + 2 * g, 2), :].rearrange(
                                     "c p h u v -> c p h (u v)")).then_inc(h_in[b], 16)

            def load_x(i, b):
                q, st = i // NS, i % NS
                at_least(sp, x1_dn, 2 * (i - 1))
                for g in range(G):
                    sp.dma_start(xt[32 * g:32 * g + C, 2 * b:2 * b + 2, :],
                                 x[bass.ds(8 * q + 2 * g, 2), :, bass.ts(st, SR), :].rearrange("u c h w -> c u (h w)")
                                 ).then_inc(x_in[b], 16)

            def store_x1(i, b):
                sp.wait_ge(x1_dn, 2 * (i + 1))
                for g in range(G):
                    sp.dma_start(x1_d[i, g, :, :].rearrange("(u c) l -> c u l", u=2),
                                 x1o[32 * g:32 * g + C, 2 * b:2 * b + 2, :]).then_inc(x1_out[b], 16)

            for b in range(2):
                load_h(b, b)
            for b in range(2):
                load_x(b, b)
            load_h(2, 0)
            with sp.Fori(0, NI // 2 - 2) as j:
                for b in range(2):
                    load_h(2 * j + (b + 3), 1 - b)
                    store_x1(2 * j + b, b)
                    load_x(2 * j + (b + 2), b)
            load_h(NI - 1, 1)
            for b in range(2):
                store_x1(NI - 4 + b, b)
                load_x(NI - 2 + b, b)

            def load_iter(i, b):
                at_least(sp, s["fc1_mm"], 2 * (i - 1))
                for g in range(G):
                    sp.dma_start(x1t[32 * g:32 * g + C, b, :, :],
                                 x1_d[i, g, :, :].rearrange("(u c) l -> c u l", u=2)).then_inc(x1t_in[b], 16)

            def load_res(i, b):
                at_least(sp, s["fin_done"], 2 * (i - 1))
                for h in range(2):
                    sp.dma_start(x1r[64 * h:64 * h + 2 * C, b, :, :],
                                 x1_d[i, h:G:2, :, :].rearrange("g p l -> p g l")).then_inc(x1r_in[b], 16)

            def store_iter(i, b):
                q, st = i // NS, i % NS
                sp.wait_ge(s["fin_done"], 2 * (i + 1))
                for h in range(2):
                    for gp in range(2):
                        dst = out[bass.ds(8 * q + 4 * gp + 2 * h, 2), :, bass.ts(st, SR), :]
                        sp.dma_start(dst.rearrange("b c h w -> (b c) (h w)"), outs[64 * h:64 * h + 2 * C, b, gp, :]
                                     ).then_inc(final_out[b], 16)

            for b in range(2):
                sp.wait_ge(x1_out[b], 16 * G * (NI // 2 - 1))
                sp.wait_ge(ctr_d, NSTEP - 2 + 2 * b)
                load_iter(b, b)
                store_x1(NI - 2 + b, b)
            for b in range(2):
                load_res(b, b)
            load_iter(2, 0)
            for b in range(2):
                sp.wait_ge(x1_out[b], 16 * G * (NI // 2))
            with sp.Fori(0, NI // 2 - 2) as j:
                for b in range(2):
                    load_iter(2 * j + (b + 3), 1 - b)
                    store_iter(2 * j + b, b)
                    load_res(2 * j + (b + 2), b)
            load_iter(NI - 1, 1)
            for b in range(2):
                store_iter(NI - 4 + b, b)
                load_res(NI - 2 + b, b)
            for b in range(2):
                store_iter(NI - 2 + b, b)
            for b in range(2):
                sp.wait_ge(final_out[b], 64 * (NI // 2))

        @block.gpsimd
        def _(pool):
            for b in range(NCB):
                nc.gpsimd.memset(xrow[b][:, :, :], 0.0).then_inc(conv_zeroed, 1)
            nc.gpsimd.memset(mhalf[:, :], -0.5).then_inc(mhalf_set, 1)
            nc.gpsimd.memset(rse[:, :, :, :, :], 0.0)
            nc.gpsimd.memset(rne[:, :, :, :], 1.0)
            for t in (ht, xt):
                last = nc.gpsimd.memset(t[:, :, :], 0.0)
            last.then_inc(zeroed, 1)
            nc.gpsimd.memset(xam[:, :, :, :, :, :], 0.0)
            nc.gpsimd.memset(pb[:, :, :, :, :], 0.0).then_inc(zeroed, 1)
            pool.wait_ge(mhalf_set, 1)

            def inv_std(m):
                pool.wait_ge(ve_d, m + 1)
                at_least(pool, rse_d, m)
                nc.gpsimd.tensor_tensor(rs[:, :], ve[:, :], mhalf[0:LB, 0:NBLK * G], ALU.pow).then_inc(pow_d, 1)

            inv_std(0)
            with pool.Fori(1, NSTEP) as m:
                inv_std(m)

            def inv_norm(i):
                pool.wait_ge(s["nv_done"], i + 1)
                at_least(pool, s["rne_done"], i)
                nc.gpsimd.tensor_tensor(rn[:, :], nv[:, :], mhalf[:, :], ALU.pow).then_inc(s["rn_done"], 1)

            def add_q(n, k):
                pool.wait_ge(s["q_done"], n + 1)
                pool.wait_ge(s["node_done"], n + 1)
                at_least(pool, s["geg_done"], n)
                nc.gpsimd.tensor_tensor(hq[:, :, :, :].rearrange("p h g i -> p h (g i)"),
                                        red9[:, :, :, :].rearrange("p h g i -> p h (g i)"),
                                        qs[:, k, :, :].rearrange("p g i -> p (g i)").unsqueeze(1).broadcast_to(
                                            [2 * O, 2, G * NN]), ALU.add).then_inc(s["addq_done"], 1)

            def some_onehot(n, k):
                for t in range(NB - NBP, NB):
                    last = nc.gpsimd.tensor_scalar(onehot[:, k, :, t, :], slot[:, k, :, :], float(t + 1 - 99), None,
                                                   ALU.is_equal)
                last.then_inc(s["onehot_pool"], 1)

            def scale_y(i, b, k):
                lo, hi = ((0, 4), (4, WX))[k]
                pool.wait_ge(s["rnt_done"], 2 * i + (k + 1))
                nc.gpsimd.tensor_tensor(xa[:, b, lo:hi, :, :].rearrange("p w u i -> p (w u i)"),
                                        rnt[:, lo:hi, :, :].rearrange("p w u i -> p (w u i)"),
                                        yb[:, b, lo:hi, :, :].rearrange("p w u i -> p (w u i)"), ALU.mult
                                        ).then_inc(s["xa_done"], 1)

            def add_x(i, b, old, gp):
                if gp == 0:
                    pool.wait_ge(x1r_in[b], 32 * (old + 1))
                pool.wait_ge(s["fc2_out"], 2 * i + (gp + 1))
                nc.gpsimd.tensor_tensor(outs[:, b, gp, :], outs[:, b, gp, :], x1r[:, b, gp, :], ALU.add
                                        ).then_inc(s["fin_done"], 1)

            def pool_slot(n, i, j, r, add=True, ahead1=True, pre=True, post=True):
                wx, b = r % WX, r // WX
                if pre and wx == 2:
                    scale_y(i + 1, (b + 1) % 2, 0)
                if ahead1 and NBP:
                    pool.wait_ge(s["slot_done"], n + 2)
                if add:
                    add_q(n - 1, (r + 1) % 2)
                if pre and wx == 2:
                    scale_y(i + 1, (b + 1) % 2, 1)
                if ahead1 and NBP:
                    some_onehot(n + 1, (r + 1) % 2)
                if pre and wx == 0:
                    inv_norm(i + 1)
                if post and wx in (5, 6):
                    add_x(i - 1, (b + 1) % 2, j, wx - 5)

            inv_norm(0)
            for k in range(2):
                scale_y(0, 0, k)
            pool_slot(-1, -1, -1, 2 * WX - 1, add=False, pre=False, post=False)
            for n in range(3 * WX):
                pool_slot(n, n // WX, (n - WX) // (2 * WX), n % (2 * WX), add=n > 0, post=n >= WX)
            with pool.Fori(1, NI // 2 - 1) as j:
                for r in range(WX, 3 * WX):
                    pool_slot(2 * WX * j + r, 2 * j + r // WX, j, r % (2 * WX))
            for n in range(NU - WX, NU):
                pool_slot(n, NI - 1, NI // 2 - 1, n % (2 * WX), ahead1=n + 1 < NU, pre=False)
            add_q(NU - 1, 1)
            for gp in range(2):
                add_x(NI - 1, 1, NI // 2 - 1, gp)

        @block.scalar
        def _(act):
            act.wait_ge(par_in, 16)
            def conv_leave(j, b):
                act.wait_ge(conv_mm, NCB * j + (b + 1))
                at_least(act, conv_out[b], 32 * j)
                nc.scalar.activation(cvo[b][:, 0:CL], bank[0:KC, 2 * b, 0:CL], ACT.Identity,
                                     bias=P("conv_b")[0:KC, bass.ds(NCB * j + b, 1)], scale=1.0
                                     ).then_inc(conv_evac_a, 1)

            for b in range(NCB):
                conv_leave(0, b)
            with act.Fori(1, C // NCB) as j:
                for b in range(NCB):
                    conv_leave(j, b)

            def square(m, r):
                act.wait_ge(ctr_d, m + 1)
                nc.scalar.activation(sq[:, :], bank[:, 0, 0:L], ACT.Square).then_inc(sq_d, 1)
                at_least(act, hn_d, m - NBUF + 1)
                nc.scalar.copy(hcs[:, r % NBUF, :], bank[:, 0, 0:L]).then_inc(hcs_d, 1)

            def gelu(m, r):
                for t in range(3):
                    act.wait_ge(mm1_d, 3 * m + (t + 1))
                    nc.scalar.activation(gl[:, t, :], bank[:, 3 + t, 0:L], ACT.Gelu, bias=b1s[:, t:t + 1], scale=1.0
                                         ).then_inc(gelu_d, 1)

            act.wait_ge(ready, 1)
            act.wait_ge(zeroed, 2)
            for m in range(3):
                square(m, m)
            for m in range(NBUF):
                square(m + 3, m + 3)
                gelu(m, m)
            with act.Fori(1, NSTEP // NBUF - 1) as j:
                for r in range(NBUF):
                    square(NBUF * j + (r + 3), r + 3)
                    gelu(NBUF * j + r, r)
            def make_y(i, b, banks=(6, 7)):
                for u in range(2):
                    act.wait_ge(s["fc1_mm"], 2 * i + (u + 1))
                    nc.scalar.activation(yb[:, b, :, u, :], bank[:, banks[u], 0:L].rearrange("p (w i) -> p w i", w=WX),
                                         ACT.Identity, bias=c1[:, 0:1],
                                         scale=P("s1")).then_inc(s["y_done"], 1)

            def square_y(i, b):
                act.wait_ge(s["y_done"], 2 * (i + 1))
                nc.scalar.activation(sq2[:, :], yb[:, b, :, :, :].rearrange("p w u i -> p (w u i)"), ACT.Square
                                     ).then_inc(s["ysq_done"], 1)

            def square_xa(i, b):
                act.wait_ge(s["xa_done"], 2 * (i + 1))
                nc.scalar.activation(sq2[:, :], xa[:, b, :, :, :].rearrange("p w u i -> p (w u i)"), ACT.Square
                                     ).then_inc(s["xasq_done"], 1)

            def take_norm(i, k, banks=(6, 7)):
                lo, hi = ((0, 4), (4, WX))[k]
                act.wait_ge(s["rn_mm"], 2 * i + (k + 1))
                nc.scalar.copy(rnt[:, lo:hi, :, :].rearrange("p w u i -> p (w u i)"),
                               bank[:, banks[k], 0:(hi - lo) * 2 * NN]).then_inc(s["rnt_done"], 1)

            def take_xb(i, b, u):
                act.wait_ge(s["half_mm"], 2 * i + (u + 1))
                nc.scalar.copy(xb[:, b, :, :, :].rearrange("p w u i -> p (w u i)")[:, u * L:(u + 1) * L],
                               bank[:, 6 + u, 0:L]).then_inc(s["xb_done"], 1)

            def spread_xa(i, b, g):
                at_least(act, s["dist_mm"], WX * (i - 1))
                nc.scalar.copy(xam[32 * g:32 * g + 32, b, :, :, g, :].rearrange("p w u i -> p (w u) i"),
                               xa[32 * g:32 * g + 32, b, :, :, :].rearrange("p w u i -> p (w u) i")
                               ).then_inc(s["xam_done"], 1)

            def fc2_leave(i, b, old, gp):
                act.wait_ge(s["fc2_mm"], 2 * (2 * i + (gp + 1)))
                if gp == 0:
                    at_least(act, final_out[b], 64 * old)
                nc.scalar.activation(outs[:, b, gp, :], bank[:, 6 + gp, 0:L], ACT.Identity, bias=c2[:, 0:1], scale=1.0
                                     ).then_inc(s["fc2_out"], 1)

            def split(n, k, part, waits, done):
                act.wait_ge(waits, n + 1)
                src = bank[:, 3, 0:G * O].rearrange("p (g o) -> p g o", g=G)
                for u in range(2):
                    last = nc.scalar.copy(pb[64 * u:64 * u + 64, k, part, :, u * O:(u + 1) * O],
                                          src[64 * u:64 * u + 64, :, :])
                last.then_inc(done, 1)

            def act_slot(n, i, j, r, gather=True, add=True, ahead1=True, ahead2=True, pre=True, post=True, early=True):
                wx, b = r % WX, r // WX
                if ahead1:
                    split(n + 1, (r + 1) % 2, 0, s["p_mm"], s["hi_done"])
                if pre and wx == 0:
                    square_y(i + 1, (b + 1) % 2)
                if ahead1:
                    split(n + 1, (r + 1) % 2, 1, s["res1_mm"], s["mid_done"])
                if pre and wx == 2:
                    take_norm(i + 1, 1)
                if ahead2:
                    act.wait_ge(s["mt_mm"], n + 3)
                    nc.scalar.copy(mts[:, :], bank[:, 4, 0:G * NN]).then_inc(s["mts_done"], 1)
                if ahead1:
                    split(n + 1, (r + 1) % 2, 2, s["res2_mm"], s["lo_done"])
                if pre and wx == 2:
                    square_xa(i + 1, (b + 1) % 2)
                if pre and wx == 3:
                    take_xb(i + 1, (b + 1) % 2, 0)
                if add:
                    act.wait_ge(s["addq_done"], n)
                    at_least(act, s["og_done"], n - 1)
                    nc.scalar.activation(gg[:, :, :, :], hq[:, :, :, :], ACT.Gelu, bias=gb[0:2 * O, 0:1], scale=1.0
                                         ).then_inc(s["geg_done"], 1)
                if gather:
                    act.wait_ge(s["self_mm"], n + 1)
                    at_least(act, s["addq_done"], n - 1)
                    nc.scalar.copy(qs[:, r % 2, :, :].rearrange("p g i -> p (g i)"), bank[0:2 * O, 5, G * NN:2 * G * NN]
                                   ).then_inc(s["q_done"], 1)
                if ahead2:
                    act.wait_ge(s["slot_mm"], n + 3)
                    at_least(act, s["onehot_done"], n + 1)
                    if NBP:
                        at_least(act, s["onehot_pool"], n + 1)
                    nc.scalar.copy(slot[:, r % 2, :, :].rearrange("p g i -> p (g i)"), bank[:, 4, G * NN:2 * G * NN]
                                   ).then_inc(s["slot_done"], 1)
                if pre and wx in (2, 3):
                    for g in (2 * wx - 4, 2 * wx - 3):
                        spread_xa(i + 1, (b + 1) % 2, g)
                if pre and wx == 1:
                    take_norm(i + 1, 0)
                if pre and wx == 3:
                    take_xb(i + 1, (b + 1) % 2, 1)
                if post and wx in (4, 5):
                    fc2_leave(i - 1, (b + 1) % 2, j, wx - 4)
                if early and wx == 6:
                    make_y(i + 2, b)

            for m in range(NSTEP - NBUF, NSTEP):
                if m + 3 < NSTEP:
                    square(m + 3, m + 3)
                gelu(m, m)
                if m == NSTEP - 3:
                    make_y(0, 0, banks=EARLY)
                    square_y(0, 0)
            for k in range(2):
                take_norm(0, k, banks=EARLY)
            square_xa(0, 0)
            for u in range(2):
                take_xb(0, 0, u)
            for g in range(G):
                spread_xa(0, 0, g)
            act_slot(-2, -1, -1, 12, gather=False, add=False, ahead1=False, pre=False, post=False)
            act_slot(-1, -1, -1, 13, gather=False, add=False, pre=False, post=False)
            for n in range(3 * WX):
                act_slot(n, n // WX, (n - WX) // (2 * WX), n % (2 * WX), add=n > 0, post=n >= WX)
            with act.Fori(1, NI // 2 - 2) as j:
                for r in range(WX, 3 * WX):
                    act_slot(2 * WX * j + r, 2 * j + r // WX, j, r % (2 * WX))
            for n in range(NU - 3 * WX, NU):
                i = n // WX
                act_slot(n, i, (i - 1) // 2, n % (2 * WX), ahead1=n + 1 < NU, ahead2=n + 2 < NU, pre=i + 1 < NI,
                         early=i + 2 < NI)
            act_slot(NU, NI, 0, 0, gather=False, ahead1=False, ahead2=False, pre=False, post=False)
            for gp in range(2):
                fc2_leave(NI - 1, 1, NI // 2 - 1, gp)

        @block.vector
        def _(dve):

            for b in range(NCB):
                nc.vector.memset(toep[b][:, :, :], 0.0).then_inc(toep_zeroed, 1)

            def duplicate(j, b):
                dve.wait_ge(conv_in[b], 80 * (j + 1))
                nc.vector.tensor_copy(xrow[b][64:64 + HW, :, 0:HW + 2 * PAD - 1], xrow[b][0:HW, :, 1:HW + 2 * PAD]
                                      ).then_inc(conv_dup, 1)

            def conv_leave(j, b):
                dve.wait_ge(conv_mm, NCB * j + (b + 1))
                at_least(dve, conv_out[b], 32 * j)
                nc.vector.tensor_scalar(cvo[b][:, CL:2 * CL], bank[0:KC, 2 * b + 1, 0:CL],
                                        P("conv_b")[0:KC, bass.ds(NCB * j + b, 1)], None, ALU.add
                                        ).then_inc(conv_evac_v, 1)

            for b in range(NCB):
                duplicate(0, b)
            dve.wait_ge(par_in, 16)
            conv_leave(0, 0)

            def conv_round(j):
                for b in range(NCB):
                    duplicate(j, b)
                    if b < NCB - 1:
                        conv_leave(j - 1, b + 1)
                    else:
                        conv_leave(j, 0)

            conv_round(1)
            with dve.Fori(2, C // NCB) as j:
                conv_round(j)
            for b in range(1, NCB):
                conv_leave(C // NCB - 1, b)

            dve.wait_ge(lnb_dot, 1)
            nc.vector.tensor_tensor(b1s[:, :], bank[:, 6, 0:3], P("b1"), ALU.add)
            nc.vector.tensor_scalar(w1g[:, :, :].rearrange("p t m -> p (t m)"), P("w1"), P("ln_g"), None, ALU.mult)
            for t in range(3):
                nc.vector.tensor_tensor(w2s[:, t, :], P("w2")[:, 128 * t:128 * t + 128], P("ls_row"), ALU.mult)
            nc.vector.tensor_tensor(b2s[:, :], P("b2"), P("ls"), ALU.mult)
            nc.vector.scalar_tensor_tensor(c1[:, :], P("b1f"), P("s1"), P("t1"), ALU.mult, ALU.add)
            nc.vector.tensor_tensor(wp[:, :].rearrange("p (g o) -> p g o", g=G), P("wb").rearrange("p (g o) -> p g o", g=G),
                                    P("es_row").unsqueeze(1).broadcast_to([128, G, O]), ALU.mult)
            wqf = wq[:, :, :, :].rearrange("p g u m -> p (g u m)")
            nc.vector.tensor_tensor(wqf, P("wa_q"), P("wb_q"), ALU.subtract).then_inc(wq_set, 1)
            dve.wait_ge(wq_set, 1)
            wqv = wq[:, :, :, :].rearrange("p g u (v o) -> p (g u v) o", v=2)
            nc.vector.tensor_tensor(wqv, wqv, P("es_row").unsqueeze(1).broadcast_to([128, 4 * G, O]), ALU.mult)
            nc.vector.scalar_tensor_tensor(gb[:, :], P("eb"), P("es"), P("et"), ALU.mult, ALU.add)
            nc.vector.tensor_tensor(f2[:, :], P("fc2"), P("s2_row"), ALU.mult)
            nc.vector.scalar_tensor_tensor(c2[:, :], P("b2f"), P("s2"), P("t2"), ALU.mult, ALU.add)
            nc.vector.tensor_copy(identb[:, :], P("ident"))
            nc.vector.tensor_scalar(nidentb[:, :], P("ident"), -1.0, None, ALU.mult)
            nc.vector.tensor_scalar(unmark[:, :], P("ident"), 1.0 / TAKEN, None, ALU.mult)
            nc.vector.tensor_copy(prefb[:, :], P("prefix"))
            nc.vector.tensor_copy(negb[:, :, :], P("negi").unsqueeze(1).broadcast_to([128, G, NN]))
            nc.vector.tensor_copy(i2b[:, :], P("i2")).then_inc(ready, 1)

            dve.wait_ge(ready, 1)
            dve.wait_ge(zeroed, 1)

            def add_eps(m):
                dve.wait_ge(var_d, m + 1)
                at_least(dve, pow_d, m)
                nc.vector.tensor_scalar(ve[:, :], bank[0:LB, 2, 0:NBLK * G], 1e-5, None, ALU.add).then_inc(ve_d, 1)

            def spread_std(m, r):
                dve.wait_ge(pow_d, m + 1)
                at_least(dve, rb_d, m - 1)
                nc.vector.tensor_copy(rse[:, r % 2, :, :, 0:C].rearrange("p k g c -> p (k g) c"),
                                      rs[:, :].unsqueeze(2).broadcast_to([LB, NBLK * G, C])).then_inc(rse_d, 1)

            def normalise(m, r):
                dve.wait_ge(rb_d, m + 1)
                dve.wait_ge(hcs_d, m + 1)
                at_least(dve, mm1_d, 3 * (m - 1))
                nc.vector.tensor_tensor(hn[:, r % 2, :], bank[:, 1, 0:L], hcs[:, r % NBUF, :], ALU.mult
                                        ).then_inc(hn_d, 1)

            def residual(m, r, old):
                dve.wait_ge(mm2_d, m + 1)
                dve.wait_ge(x_in[r % NBUF // 2], 16 * G * (old + 1))
                at_least(dve, x1_out[r % NBUF // 2], 16 * G * old)
                nc.vector.scalar_tensor_tensor(x1o[:, r % NBUF, :], bank[:, 6 + r % 2, 0:L], b2s[:, 0:1],
                                               xt[:, r % NBUF, :], ALU.add, ALU.add).then_inc(x1_dn, 1)

            def mlp_slot(m, r, old, first=False):
                end = NSTEP if isinstance(m, int) else 1 << 30
                now = m if isinstance(m, int) else 0
                if not first:
                    residual(m - 1, (r - 1) % NBUF, old)
                if now + 2 < end:
                    spread_std(m + 2, r)
                if now + 1 < end:
                    normalise(m + 1, r + 1)
                if now + 3 < end:
                    add_eps(m + 3)

            add_eps(0)
            spread_std(0, 0)
            add_eps(1)
            spread_std(1, 1)
            normalise(0, 0)
            add_eps(2)
            for m in range(NBUF):
                mlp_slot(m, m, 0, first=m == 0)
            mlp_slot(NBUF, 0, 0)
            with dve.Fori(1, NSTEP // NBUF - 1) as j:
                for r in range(1, NBUF + 1):
                    mlp_slot(NBUF * j + r, r, j)
            def norms(i, banks=(6, 7)):
                dve.wait_ge(s["norm_mm"], i + 1)
                at_least(dve, s["rn_done"], i)
                nc.vector.tensor_scalar(nv[:, :], bank[:, banks[0], 0:WX * G], 1e-24, None, ALU.max).then_inc(s["nv_done"], 1)

            def spread_norm(i):
                dve.wait_ge(s["rn_done"], i + 1)
                at_least(dve, s["rn_mm"], i)
                nc.vector.tensor_copy(rne[:, :, :, 0:C].rearrange("p w g c -> p (w g) c"),
                                      rn[:, :].unsqueeze(2).broadcast_to([128, WX * G, C])).then_inc(s["rne_done"], 1)

            def dist_of(t):
                return bank[:, 2, t * NN:(t + 1) * NN]

            def top8(k):
                for t in range(G):
                    nc.vector.max(t8[:, G * k + t, :], dist_of(t)).then_inc(s["t8_done"], 1)

            def mark8(n, k):
                for t in range(G):
                    nc.vector.match_replace(marked[:, k, t, :], t8[:, G * k + t, :], dist_of(t), TAKEN
                                            ).then_inc(s["mark_done"], 1)

            def make_onehot(n, k):
                dve.wait_ge(s["slot_done"], n + 1)
                for t in range(NB - NBP):
                    last = nc.vector.tensor_scalar(onehot[:, k, :, t, :], slot[:, k, :, :], float(t + 1 - 99), None,
                                                   ALU.is_equal)
                last.then_inc(s["onehot_done"], 1)

            def reduce(n, k, g, top8s=0):
                dve.wait_ge(s["gat_mm"], G * n + (g + 1))
                src = bank[0:2 * O, g % 2, :].rearrange("p (k i) -> p i k", k=NB)
                for h, op in enumerate((ALU.max, ALU.min)):
                    if h == 1:
                        at_least(dve, s["t8_done"], top8s)
                    nc.vector.tensor_reduce(red[:, k, h, g, :], src, axis=mybir.AxisListType.X, op=op
                                            ).then_inc(s["red_done"], 1)

            def with_self(n, k):
                dve.wait_ge(s["q_done"], n + 1)
                dve.wait_ge(s["red_done"], 2 * G * (n + 1))
                at_least(dve, s["addq_done"], n)
                for h, op in enumerate((ALU.max, ALU.min)):
                    last = nc.vector.tensor_tensor(red9[:, h, :, :].rearrange("p g i -> p (g i)"),
                                                   red[:, k, h, :, :].rearrange("p g i -> p (g i)"),
                                                   bank[0:2 * O, 5, 0:G * NN], op)
                last.then_inc(s["node_done"], 1)

            def best(n, i, wx, b, first):
                dve.wait_ge(s["geg_done"], n + 1)
                if wx == 0 and not first:
                    dve.wait_ge(s["fc2_mm"], G * (i - 1))
                nc.vector.tensor_tensor(og[:, b, :, :, wx, :],
                                        gg[:, 0, :, :].rearrange("p g (r c) -> p g r c", c=WS),
                                        gg[:, 1, :, :].rearrange("p g (r c) -> p g r c", c=WS), ALU.max
                                        ).then_inc(s["og_done"], 1)

            def dve_slot(n, i, r, gather=True, ahead1=True, ahead3=True, pre=True, first=False):
                wx, b = r % WX, r // WX
                if gather and not (first and r < 2):
                    best(n - 2, i, (wx - 2) % WX, ((r - 2) % (2 * WX)) // WX, first)
                if gather:
                    reduce(n, r % 2, 0)
                    if not (first and r == 0):
                        with_self(n - 1, (r + 1) % 2)
                if ahead1:
                    make_onehot(n + 1, (r + 1) % 2)
                if gather:
                    reduce(n, r % 2, 1)
                if pre and wx == 0:
                    norms(i + 1)
                if pre and wx == 1:
                    spread_norm(i + 1)
                if gather:
                    reduce(n, r % 2, 2)
                if ahead3:
                    if not gather:
                        dve.wait_ge(s["dist_mm"], n + 4)
                    top8((r + 1) % 2)
                    if not gather:
                        dve.wait_ge(s["t8_done"], G * (n + 4))
                if gather:
                    reduce(n, r % 2, 3, top8s=G * (n + 4) if ahead3 else 0)
                if ahead3:
                    mark8(n + 3, (r + 1) % 2)

            for m in range(NSTEP - NBUF + 1, NSTEP):
                mlp_slot(m, m % NBUF, (m - 1) // NBUF)
                if m == NSTEP - 2:
                    norms(0, banks=EARLY)
            spread_norm(0)
            residual(NSTEP - 1, NBUF - 1, NSTEP // NBUF - 1)

            for n in (-3, -2, -1):
                dve_slot(n, -1, n + 2 * WX, gather=False, ahead1=False, pre=False)
            make_onehot(0, 0)
            for n in range(3 * WX):
                dve_slot(n, n // WX, n % (2 * WX), first=n < 2 * WX)
            with dve.Fori(1, NI // 2 - 1) as j:
                for r in range(WX, 3 * WX):
                    dve_slot(2 * WX * j + r, 2 * j + r // WX, r % (2 * WX))
            for n in range(NU - WX, NU):
                dve_slot(n, NI - 1, n % (2 * WX), ahead1=n + 1 < NU, ahead3=n + 3 < NU, pre=False)
            with_self(NU - 1, 1)
            for n in (NU - 2, NU - 1):
                best(n, NI - 1, n % WX, 1, False)

        @block.tensor
        def _(pe):
            mm = nc.tensor.matmul

            def conv_channel(j, b):
                pe.wait_ge(conv_dup, NCB * j + (b + 1))
                at_least(pe, conv_evac_a, NCB * j + (b - NCB + 1))
                at_least(pe, conv_evac_v, NCB * j + (b - NCB + 1))
                for sh in range(NSH):
                    for ch in range(2):
                        last = mm(bank[0:KC, 2 * b + ch, 0:CL].rearrange("p (b v) -> p b v", v=W2), toep[b][:, sh, :],
                                  xrow[b][:, ICH * ch:ICH * (ch + 1), 2 * sh:2 * sh + HW - 1:2],
                                  start=sh == 0, stop=sh == NSH - 1)
                last.then_inc(conv_mm, 1)

            for b in range(NCB):
                conv_channel(0, b)
            with pe.Fori(1, C // NCB) as j:
                for b in range(NCB):
                    conv_channel(j, b)

            pe.wait_ge(par_in, 16)
            pe.wait_ge(conv_evac_v, C)
            pe.wait_ge(conv_evac_a, C)
            for t in range(3):
                last = mm(bank[:, 6, t:t + 1], P("w1")[:, 128 * t:128 * t + 128], P("ln_b"), start=True, stop=True)
            last.then_inc(lnb_dot, 1)
            pe.wait_ge(ready, 1)
            pe.wait_ge(zeroed, 1)

            def centre(m, r, old):
                pe.wait_ge(h_in[r % NBUF // 2], 16 * G * (old + 1))
                at_least(pe, hcs_d, m)
                b = r % NBUF // 2
                mm(bank[:, 0, 0:L].rearrange("c (h v p) -> c h v p", p=2, v=W2), P("center"),
                   ht[:, 2 * b:2 * b + 2, :].rearrange("c a l -> c (a l)").rearrange(
                       "c (p h u v) -> c u h v p", p=2, u=2, v=W2)[:, r % 2, ::-1, :, :], start=True, stop=True
                   ).then_inc(ctr_d, 1)

            def variance(m):
                pe.wait_ge(sq_d, m + 1)
                at_least(pe, ve_d, m)
                for k in range(NBLK):
                    last = mm(bank[0:LB, 2, G * k:G * k + G], sq[:, LB * k:LB * k + LB], P("mean4"), start=True, stop=True)
                last.then_inc(var_d, 1)

            def turn_std(m, r):
                pe.wait_ge(rse_d, m + 1)
                at_least(pe, hn_d, m)
                for k in range(NBLK):
                    last = mm(bank[:, 1, LB * k:LB * k + LB], rse[:, r % 2, k, :, :].rearrange("p g c -> p (g c)"),
                              P("ident")[0:LB, 0:LB], start=True, stop=True)
                last.then_inc(rb_d, 1)

            def expand(m, r):
                pe.wait_ge(hn_d, m + 1)
                for t in range(3):
                    at_least(pe, gelu_d, 3 * (m - 1) + (t + 1))
                    mm(bank[:, 3 + t, 0:L], w1g[:, t, :], hn[:, r % 2, :], start=True, stop=True).then_inc(mm1_d, 1)

            def contract(m, r):
                at_least(pe, x1_dn, m - 1)
                for t in range(3):
                    pe.wait_ge(gelu_d, 3 * m + (t + 1))
                    last = mm(bank[:, 6 + r % 2, 0:L], w2s[:, t, :], gl[:, t, :], start=t == 0, stop=t == 2)
                last.then_inc(mm2_d, 1)

            def mlp_slot(m, r, j, first=False):
                end = NSTEP if isinstance(m, int) else 1 << 30
                now = m if isinstance(m, int) else 0
                if not first:
                    contract(m - 1, r - 1)
                if now + 3 < end:
                    centre(m + 3, r + 3, j + (r + 3) // NBUF)
                expand(m, r)
                if now + 1 < end:
                    turn_std(m + 1, r + 1)
                if now + 3 < end:
                    variance(m + 3)

            for m in range(3):
                centre(m, m, 0)
                variance(m)
            turn_std(0, 0)
            for m in range(NBUF):
                mlp_slot(m, m, 0, first=m == 0)
            with pe.Fori(1, NSTEP // NBUF - 1) as j:
                for r in range(NBUF):
                    mlp_slot(NBUF * j + r, r, j)
            def fc1(i, b, old, u, banks=(6, 7)):
                if u == 0:
                    pe.wait_ge(x1t_in[b], 64 * (old + 1))
                at_least(pe, s["fc2_out"], 2 * (i - 2) + (u - 1))
                mm(bank[:, banks[u], 0:L].rearrange("p (w r c) -> p w r c", w=WX, c=WS), P("fc1"),
                   x1t[:, b, u, :].rearrange("p (r w c) -> p w r c", w=WX, c=WS), start=True, stop=True
                   ).then_inc(s["fc1_mm"], 1)

            def norm(i, banks=(6, 7)):
                pe.wait_ge(s["ysq_done"], i + 1)
                for w in range(WX):
                    last = mm(bank[:, banks[0], G * w:G * w + G], sq2[:, 128 * w:128 * w + 128], P("norm4"), start=True, stop=True)
                last.then_inc(s["norm_mm"], 1)

            def turn_norm(i, windows, banks=(6, 7)):
                pe.wait_ge(s["rne_done"], i + 1)
                for w in windows:
                    last = mm(bank[:, banks[w // 4], 128 * (w % 4):128 * (w % 4) + 128],
                              rne[:, w, :, :].rearrange("p g c -> p (g c)"), P("ident"), start=True, stop=True)
                    if w in (3, WX - 1):
                        last.then_inc(s["rn_mm"], 1)

            def halfsq(i, b, u, part):
                if part == 0:
                    at_least(pe, s["rnt_done"], 2 * (i + 1))
                    pe.wait_ge(s["xa_done"], 2 * (i + 1))
                    mm(bank[:, 6 + u, 0:L], P("chan"), xa[:, b, :, :, :].rearrange("p w u i -> p (w u i)")[:, L * u:L * u + L],
                       start=True, stop=False)
                else:
                    pe.wait_ge(s["xasq_done"], i + 1)
                    mm(bank[:, 6 + u, 0:L], P("halfsq"), sq2[:, L * u:L * u + L], start=False, stop=True
                       ).then_inc(s["half_mm"], 1)

            def fc2(i, b, g):
                if g == 0:
                    pe.wait_ge(s["og_done"], WX * (i + 1))
                    at_least(pe, s["xb_done"], 2 * (min(i + 3, NI) if isinstance(i, int) else i + 3))
                mm(bank[64 * (g % 2):64 * (g % 2) + 64, 6 + g // 2, 0:L], f2[0:2 * O, :],
                   og[:, b, g, :, :, :].rearrange("p r w c -> p (r w c)"), start=True, stop=True
                   ).then_inc(s["fc2_mm"], 1)

            def dist(n, i, b, wx):
                pe.wait_ge(s["xb_done"], 2 * (i + 1))
                pe.wait_ge(s["xam_done"], G * (i + 1))
                at_least(pe, s["mark_done"], G * n)
                mm(bank[:, 2, 0:G * NN], identb[:, :], negb[:, :, :].rearrange("p g i -> p (g i)"), start=True,
                   stop=False, skip_group_check=True)
                for gp in range(2):
                    for u in range(2):
                        t = 2 * gp + u
                        last = mm(bank[:, 2, t * NN:(t + 1) * NN],
                                  xam[:, b, wx, u, 2 * gp:2 * gp + 2, :].rearrange("p g i -> p (g i)"),
                                  xb[:, b, wx, u, :], start=False, stop=True, skip_group_check=True)
                last.then_inc(s["dist_mm"], 1)

            def project(n, i, b, wx):
                pe.wait_ge(s["y_done"], 2 * (i + 1))
                at_least(pe, s["lo_done"], n)
                both = yb[:, b, wx, :, :].rearrange("p u i -> p (u i)")
                mm(bank[:, 3, 0:G * O], both, wp[:, :], start=True, stop=False, skip_group_check=True
                   ).then_inc(s["p_mm"], 1)

            def subtract(n, k, part, waits, done):
                pe.wait_ge(waits, n + 1)
                for u in range(2):
                    last = mm(bank[:, 3, 0:G * O].rearrange("p (g o) -> p g o", g=G), nidentb[:, :],
                              pb[:, k, part, :, u * O:(u + 1) * O], start=False, stop=part == 1 and u == 1,
                              skip_group_check=True)
                last.then_inc(done, 1)

            def transpose(n, k):
                pe.wait_ge(s["mark_done"], G * (n + 1))
                at_least(pe, s["slot_done"], n)
                for gp in range(2):
                    last = mm(bank[:, 4, 128 * gp:128 * gp + 128],
                              marked[:, k, 2 * gp:2 * gp + 2, :].rearrange("p u j -> p (u j)"), unmark[:, :],
                              start=True, stop=True)
                last.then_inc(s["mt_mm"], 1)

            def ranks(n):
                pe.wait_ge(s["mts_done"], n + 1)
                mm(bank[:, 4, 256:512], prefb[:, :], mts[:, :], start=True, stop=True).then_inc(s["slot_mm"], 1)

            def gather(n, k, g):
                if g == 0:
                    pe.wait_ge(s["onehot_done"], n + 1)
                    if NBP:
                        pe.wait_ge(s["onehot_pool"], n + 1)
                    pe.wait_ge(s["lo_done"], n + 1)
                at_least(pe, s["red_done"], 2 * (G * n + (g - 1)))
                for part in range(3):
                    last = mm(bank[0:2 * O, g % 2, :], pb[:, k, part, g, :],
                              onehot[:, k, g, :, :].rearrange("p k i -> p (k i)"), start=part == 0, stop=part == 2)
                last.then_inc(s["gat_mm"], 1)

            def self_and_q(n, k, b, wx, groups):
                at_least(pe, s["node_done"], n)
                at_least(pe, s["q_done"], n)
                for g in groups:
                    for part in range(3):
                        mm(bank[0:2 * O, 5, g * NN:(g + 1) * NN], pb[:, k, part, g, :], i2b[:, :], start=part == 0,
                           stop=part == 2)
                    for u in range(2):
                        last = mm(bank[0:2 * O, 5, (G + g) * NN:(G + g + 1) * NN], wq[:, g, u, :],
                                  yb[:, b, wx, u, :], start=u == 0, stop=u == 1)
                    if g == G - 1:
                        last.then_inc(s["self_mm"], 1)

            def pe_slot(n, i, j, r, gath=True, ahead1=True, ahead2=True, ahead3=True, pre=True, post=True, early=True):
                wx, b, k = r % WX, r // WX, r % 2
                r2, r3 = (r + 2) % (2 * WX), (r + 3) % (2 * WX)
                bn = (b + 1) % 2
                if pre and wx == 2:
                    turn_norm(i + 1, (4,))
                if pre and wx == 3:
                    halfsq(i + 1, bn, 0, 0)
                if gath:
                    gather(n, k, 1)
                if ahead1:
                    subtract(n + 1, 1 - k, 0, s["hi_done"], s["res1_mm"])
                if ahead3:
                    dist(n + 3, i + (wx + 3) // WX, r3 // WX, r3 % WX)
                if pre and wx == 0:
                    norm(i + 1)
                if pre and wx == 2:
                    turn_norm(i + 1, (5, 6))
                if pre and wx == 3:
                    halfsq(i + 1, bn, 0, 1)
                if post and wx in (4, 5):
                    fc2(i - 1, bn, 2 * wx - 8)
                if early and wx == 6:
                    fc1(i + 2, b, j + 1, 0)
                if gath:
                    gather(n, k, 2)
                if ahead2:
                    transpose(n + 2, k)
                if ahead1:
                    subtract(n + 1, 1 - k, 1, s["mid_done"], s["res2_mm"])
                if gath:
                    self_and_q(n, k, b, wx, range(2))
                    gather(n, k, 3)
                if ahead2:
                    ranks(n + 2)
                if gath:
                    self_and_q(n, k, b, wx, range(2, G))
                if pre and wx == 1:
                    turn_norm(i + 1, (0, 1))
                if pre and wx == 3:
                    halfsq(i + 1, bn, 1, 0)
                if post and wx in (4, 5):
                    fc2(i - 1, bn, 2 * wx - 7)
                if early and wx == 6:
                    fc1(i + 2, b, j + 1, 1)
                if ahead2:
                    project(n + 2, i + (wx + 2) // WX, r2 // WX, r2 % WX)
                if ahead1:
                    gather(n + 1, 1 - k, 0)
                if pre and wx == 1:
                    turn_norm(i + 1, (2, 3))
                if pre and wx == 3:
                    halfsq(i + 1, bn, 1, 1)

            pe.wait_ge(zeroed, 2)
            for r in range(NBUF):
                mlp_slot(NSTEP - NBUF + r, r, NSTEP // NBUF - 1)
                if r == NBUF - 3:
                    pe.wait_ge(hcs_d, NSTEP)
                    pe.wait_ge(ve_d, NSTEP)
                    for u in range(2):
                        fc1(0, 0, 0, u, banks=EARLY)
                if r == NBUF - 2:
                    norm(0, banks=EARLY)
            contract(NSTEP - 1, NSTEP - 1)
            turn_norm(0, range(WX), banks=EARLY)
            pe.wait_ge(x1_dn, NSTEP)
            for u in range(2):
                halfsq(0, 0, u, 0)
                halfsq(0, 0, u, 1)
            pe_slot(-3, -1, -1, 11, gath=False, ahead1=False, ahead2=False, pre=False, post=False)
            pe_slot(-2, -1, -1, 12, gath=False, ahead1=False, pre=False, post=False)
            pe_slot(-1, -1, -1, 13, gath=False, pre=False, post=False)
            for r in range(2 * WX):
                pe_slot(r, r // WX, 0, r, post=r >= WX)
            with pe.Fori(1, NI // 2 - 1) as j:
                for r in range(2 * WX):
                    pe_slot(2 * WX * j + r, 2 * j + r // WX, j, r)
            for r in range(2 * WX):
                n = NU - 2 * WX + r
                pe_slot(n, NI - 2 + r // WX, NI // 2 - 1, r, ahead1=n + 1 < NU, ahead2=n + 2 < NU, ahead3=n + 3 < NU,
                        pre=r < WX, early=False)
            for g in range(G):
                fc2(NI - 1, 1, g)


def kernel(**inputs):
    import numpy as np
    import concourse.bacc as bacc
    from concourse import mybir as mb
    from concourse.bass_utils import run_bass_kernel_spmd

    a = {k: np.asarray(v) for k, v in inputs.items()}
    par = np.zeros((128, NCOL), np.float32)

    def P(name):
        at, n = COLS[name]
        return par[:, at:at + n]

    for g in range(G):
        r = slice(32 * g, 32 * g + C)
        P("center")[r, r] = np.eye(C) - 1.0 / C
        P("mean4")[r, g] = 1.0 / C
        P("norm4")[r, g] = 1.0
        P("halfsq")[r, 32 * g + C] = -0.5
        P("chan")[r, r] = np.eye(C)
    P("ident")[:] = np.eye(128)
    for u in range(2):
        r = slice(NN * u, NN * u + NN)
        P("prefix")[r, r] = np.triu(np.ones((NN, NN))) - 99.0 * np.eye(NN)
        P("negi")[r] = NEG * np.eye(NN)
        P("i2")[r] = np.eye(NN)
    w1, w2 = a["L0_conv_w1"], a["L0_conv_w2"]
    fc1, ew, fc2 = a["L1_conv_fc1_w"], a["L1_conv_ew"], a["L1_conv_fc2_w"]
    for g in range(G):
        r = slice(32 * g, 32 * g + C)
        P("w1")[r, F * g:F * (g + 1)] = w1
        for f in range(F):
            t, p = divmod(F * g + f, 128)
            P("w2")[p, 128 * t + 32 * g:128 * t + 32 * g + C] = w2[f]
            P("b1")[p, t] = a["L0_conv_b1"][f]
        P("ls_row")[:, r] = a["L0_conv_layer_scale"].reshape(1, C)
        for name, v in (("ln_g", "L0_conv_ln_g"), ("ln_b", "L0_conv_ln_b"), ("b2", "L0_conv_b2"),
                        ("ls", "L0_conv_layer_scale"), ("s1", "L1_conv_fc1_s"), ("b1f", "L1_conv_fc1_b"),
                        ("t1", "L1_conv_fc1_t")):
            P(name)[r, 0] = a[v].reshape(C)
        P("t1")[32 * g + C, 0] = 1.0
        P("fc1")[r, r] = fc1.T
        P("wb")[r, O * g:O * (g + 1)] = ew[:, C:].T
        for u in range(2):
            c = ((g * 2 + u) * 2 + u) * O
            P("wa_q")[r, c:c + O] = ew[:, :C].T
            P("wb_q")[r, c:c + O] = ew[:, C:].T
    P("conv_b")[:] = a["L0_conv_conv_b"].reshape(1, C)
    P("es_row")[:] = a["L1_conv_es"].reshape(1, O)
    for k in range(2):
        r = slice(O * k, O * (k + 1))
        for name in ("eb", "es", "et"):
            P(name)[r, 0] = a["L1_conv_" + name]
        P("fc2")[r, C * k:C * (k + 1)] = fc2.T
        P("s2_row")[:, C * k:C * (k + 1)] = a["L1_conv_fc2_s"].reshape(1, C)
        for h in range(2):
            r = slice(64 * h + C * k, 64 * h + C * (k + 1))
            for name, v in (("s2", "L1_conv_fc2_s"), ("b2f", "L1_conv_fc2_b"), ("t2", "L1_conv_fc2_t")):
                P(name)[r, 0] = a[v]
    z = np.zeros((C, KS, ZL), np.float32)
    z[:, :, HW - 1 - PAD:HW + PAD] = a["L0_conv_conv_w"].reshape(C, KS, KS).transpose(0, 2, 1)

    nc = bacc.Bacc("TRN2", target_bir_lowering=False, num_devices=1)
    arrays = {"x": np.ascontiguousarray(a["x"]), "zfilt": z, "params": par}
    args = [nc.dram_tensor("in_" + n, v.shape, mb.dt.float32, kind="ExternalInput").ap() for n, v in arrays.items()]
    args.append(nc.dram_tensor("out0", (B, C, HW, HW), mb.dt.float32, kind="ExternalOutput").ap())
    build(nc, *args)
    res = run_bass_kernel_spmd(nc, [{"in_" + n: v for n, v in arrays.items()}], core_ids=[0])
    return res.results[0]["out0"]
```
